# Optimizing a Trainium2 kernel written in Bass

```python
import numpy as np
import jax
import jax.numpy as jnp

def _softmax(x, axis=-1):
    return jax.nn.softmax(x, axis=axis)

def _gelu(x):
    return jax.nn.gelu(x, approximate=True)

def _silu(x):
    return jax.nn.silu(x)

def _sigmoid(x):
    return jax.nn.sigmoid(x)

def _layernorm(x, axis=-1, eps=1e-05):
    m = jnp.mean(x, axis=axis, keepdims=True)
    v = jnp.var(x, axis=axis, keepdims=True)
    return (x - m) / jnp.sqrt(v + eps)

def _scatter_add(tgt, idx, src, axis=0):
    return tgt.at[idx].add(src)

def _segment_sum(src, seg, n):
    return jax.ops.segment_sum(src, seg, n)
kernel_name = 'mk_recurrent_d2_jaxref_r8_a81fc7'

def setup_inputs(seed: int=0):
    np.random.seed(seed)
    _w = jnp.asarray

    def _L0_attn_setup():
        import jax, jax.numpy as jnp
        import numpy as np
        D = 128
        HS = 64
        H = D // HS
        B, T = (4, 256)
        EPS = 1e-05

        def _reference_tuple_inner(x, ln_g, ln_b, Wx, Ww, bw, Wk, Wv, Wr, Wo):
            Bb, Tt, C = x.shape
            nh, hs = (C // HS, HS)
            mu = x.mean(-1, keepdims=True)
            var = x.var(-1, keepdims=True)
            xn = (x - mu) / jnp.sqrt(var + EPS) * ln_g + ln_b
            w = jax.nn.sigmoid(xn @ Wx @ Ww + bw).reshape(Bb, Tt, nh, hs)
            k = (xn @ Wk).reshape(Bb, Tt, nh, hs)
            v = (xn @ Wv).reshape(Bb, Tt, nh, hs)
            r = jax.nn.sigmoid(xn @ Wr).reshape(Bb, Tt, nh, hs)

            def step(state, inp):
                kt, vt, wt, rt = inp
                state = (1.0 - wt)[..., None] * state + kt[..., None] * vt[..., None, :]
                out = jnp.einsum('bhd,bhde->bhe', rt, state)
                return (state, out)
            init = jnp.zeros((Bb, nh, hs, hs), x.dtype)
            tm = lambda a: jnp.moveaxis(a, 1, 0)
            state, outs = jax.lax.scan(step, init, (tm(k), tm(v), tm(w), tm(r)))
            y = jnp.moveaxis(outs, 0, 1).reshape(Bb, Tt, C) @ Wo
            return (y, state)
        key = jax.random.key(seed)
        ks = jax.random.split(key, 8)
        s = 1.0 / np.sqrt(D)
        mk = lambda k: jax.random.normal(k, (D, D), jnp.float32) * s
        return {'x': jax.random.normal(ks[0], (B, T, D), jnp.float32), 'ln_g': jnp.ones((D,), jnp.float32), 'ln_b': jnp.zeros((D,), jnp.float32), 'Wx': mk(ks[1]), 'Ww': mk(ks[2]), 'bw': jnp.zeros((D,), jnp.float32), 'Wk': mk(ks[3]), 'Wv': mk(ks[4]), 'Wr': mk(ks[5]), 'Wo': mk(ks[6])}
    _L0_attn_in = _L0_attn_setup()

    def _L0_ffn_setup():
        import jax, jax.numpy as jnp
        import numpy as np
        TOP_K = 2
        key = jax.random.key(seed)
        k1, k2, k3, k4 = jax.random.split(key, 4)
        B, S, D = (2, 256, 128)
        E, W = (8, 128)
        x = jax.random.normal(k1, (B, S, D), dtype=jnp.float32)
        router_w = jax.random.normal(k2, (E, D), dtype=jnp.float32) * 0.02
        w1 = jax.random.normal(k3, (D, E * W), dtype=jnp.float32) * 0.02
        w2 = jax.random.normal(k4, (E * W, D), dtype=jnp.float32) * 0.02
        return {'x': x, 'router_w': router_w, 'w1': w1, 'w2': w2}
    _L0_ffn_in = _L0_ffn_setup()

    def _L1_attn_setup():
        import jax, jax.numpy as jnp
        import numpy as np
        DIM = 128
        H = 16
        HD = DIM // H
        EPS_DENOM = 1e-06
        EPS_LN = 1e-05
        key = jax.random.key(seed)
        ks = jax.random.split(key, 8)
        B, N = (4, 512)
        s = 1.0 / np.sqrt(DIM)
        return {'x': jax.random.normal(ks[0], (B, N, DIM), dtype=jnp.float32), 'Wq': jax.random.normal(ks[1], (DIM, DIM), dtype=jnp.float32) * s, 'bq': jnp.zeros((DIM,), dtype=jnp.float32), 'Wk': jax.random.normal(ks[2], (DIM, DIM), dtype=jnp.float32) * s, 'bk': jnp.zeros((DIM,), dtype=jnp.float32), 'Wv': jax.random.normal(ks[3], (DIM, DIM), dtype=jnp.float32) * s, 'bv': jnp.zeros((DIM,), dtype=jnp.float32), 'gamma': jnp.ones((DIM,), dtype=jnp.float32), 'beta': jnp.zeros((DIM,), dtype=jnp.float32)}
    _L1_attn_in = _L1_attn_setup()

    def _L1_ffn_setup():
        import jax, jax.numpy as jnp
        import numpy as np
        DIM = 128

        def _reference_tuple_inner(x, W_r, W_k, W_v, mu_r, mu_k):
            B, T, C = x.shape
            x_prev = jnp.concatenate([jnp.zeros((B, 1, C), x.dtype), x[:, :-1, :]], axis=1)
            xr = mu_r * x + (1.0 - mu_r) * x_prev
            xk = mu_k * x + (1.0 - mu_k) * x_prev
            r = jax.nn.sigmoid(jnp.einsum('btc,dc->btd', xr, W_r))
            k = jnp.einsum('btc,dc->btd', xk, W_k)
            k_act = jnp.square(jax.nn.relu(k))
            out = r * jnp.einsum('btc,dc->btd', k_act, W_v)
            new_state = x[:, -1, :]
            return (out, new_state)
        key = jax.random.key(seed)
        ks = jax.random.split(key, 6)
        B, T, C = (8, 256, DIM)
        x = jax.random.normal(ks[0], (B, T, C), dtype=jnp.float32)
        s = 1.0 / np.sqrt(C)
        W_r = jax.random.uniform(ks[1], (C, C), jnp.float32, -s, s)
        W_k = jax.random.uniform(ks[2], (C, C), jnp.float32, -s, s)
        W_v = jax.random.uniform(ks[3], (C, C), jnp.float32, -s, s)
        mu_r = jax.random.uniform(ks[4], (C,), jnp.float32)
        mu_k = jax.random.uniform(ks[5], (C,), jnp.float32)
        return {'x': x, 'W_r': W_r, 'W_k': W_k, 'W_v': W_v, 'mu_r': mu_r, 'mu_k': mu_k}
    _L1_ffn_in = _L1_ffn_setup()
    _d = {'L0_attn_x': _L0_attn_in['x'], 'L0_attn_ln_g': _L0_attn_in['ln_g'], 'L0_attn_ln_b': _L0_attn_in['ln_b'], 'L0_attn_Wx': _L0_attn_in['Wx'], 'L0_attn_Ww': _L0_attn_in['Ww'], 'L0_attn_bw': _L0_attn_in['bw'], 'L0_attn_Wk': _L0_attn_in['Wk'], 'L0_attn_Wv': _L0_attn_in['Wv'], 'L0_attn_Wr': _L0_attn_in['Wr'], 'L0_attn_Wo': _L0_attn_in['Wo'], 'L0_ffn_router_w': _L0_ffn_in['router_w'], 'L0_ffn_w1': _L0_ffn_in['w1'], 'L0_ffn_w2': _L0_ffn_in['w2'], 'L1_attn_Wq': _L1_attn_in['Wq'], 'L1_attn_bq': _L1_attn_in['bq'], 'L1_attn_Wk': _L1_attn_in['Wk'], 'L1_attn_bk': _L1_attn_in['bk'], 'L1_attn_Wv': _L1_attn_in['Wv'], 'L1_attn_bv': _L1_attn_in['bv'], 'L1_attn_gamma': _L1_attn_in['gamma'], 'L1_attn_beta': _L1_attn_in['beta'], 'L1_ffn_W_r': _L1_ffn_in['W_r'], 'L1_ffn_W_k': _L1_ffn_in['W_k'], 'L1_ffn_W_v': _L1_ffn_in['W_v'], 'L1_ffn_mu_r': _L1_ffn_in['mu_r'], 'L1_ffn_mu_k': _L1_ffn_in['mu_k']}
    _x0 = _d['L0_attn_x']
    _d['L0_attn_x'] = jax.random.normal(jax.random.fold_in(jax.random.key(seed), 1), (32, 256, 128), dtype=_x0.dtype)
    del _x0
    return _d

def reference(L0_attn_x, L0_attn_ln_g, L0_attn_ln_b, L0_attn_Wx, L0_attn_Ww, L0_attn_bw, L0_attn_Wk, L0_attn_Wv, L0_attn_Wr, L0_attn_Wo, L0_ffn_router_w, L0_ffn_w1, L0_ffn_w2, L1_attn_Wq, L1_attn_bq, L1_attn_Wk, L1_attn_bk, L1_attn_Wv, L1_attn_bv, L1_attn_gamma, L1_attn_beta, L1_ffn_W_r, L1_ffn_W_k, L1_ffn_W_v, L1_ffn_mu_r, L1_ffn_mu_k):

    def _L0_attn_ref(x, ln_g, ln_b, Wx, Ww, bw, Wk, Wv, Wr, Wo):
        import jax, jax.numpy as jnp
        import numpy as np
        D = 128
        HS = 64
        H = D // HS
        B, T = (4, 256)
        EPS = 1e-05

        def _reference_tuple_inner(x, ln_g, ln_b, Wx, Ww, bw, Wk, Wv, Wr, Wo):
            Bb, Tt, C = x.shape
            nh, hs = (C // HS, HS)
            mu = x.mean(-1, keepdims=True)
            var = x.var(-1, keepdims=True)
            xn = (x - mu) / jnp.sqrt(var + EPS) * ln_g + ln_b
            w = jax.nn.sigmoid(xn @ Wx @ Ww + bw).reshape(Bb, Tt, nh, hs)
            k = (xn @ Wk).reshape(Bb, Tt, nh, hs)
            v = (xn @ Wv).reshape(Bb, Tt, nh, hs)
            r = jax.nn.sigmoid(xn @ Wr).reshape(Bb, Tt, nh, hs)

            def step(state, inp):
                kt, vt, wt, rt = inp
                state = (1.0 - wt)[..., None] * state + kt[..., None] * vt[..., None, :]
                out = jnp.einsum('bhd,bhde->bhe', rt, state)
                return (state, out)
            init = jnp.zeros((Bb, nh, hs, hs), x.dtype)
            tm = lambda a: jnp.moveaxis(a, 1, 0)
            state, outs = jax.lax.scan(step, init, (tm(k), tm(v), tm(w), tm(r)))
            y = jnp.moveaxis(outs, 0, 1).reshape(Bb, Tt, C) @ Wo
            return (y, state)
        return _reference_tuple_inner(x, ln_g, ln_b, Wx, Ww, bw, Wk, Wv, Wr, Wo)[0]

    def _L0_ffn_ref(x, router_w, w1, w2):
        import jax, jax.numpy as jnp
        import numpy as np
        TOP_K = 2
        B, S, D = x.shape
        E = router_w.shape[0]
        W = w1.shape[1] // E
        T = B * S
        xf = x.reshape(T, D)
        router_logits = jnp.einsum('td,ed->te', xf, router_w)
        router_probs = jax.nn.sigmoid(router_logits.astype(jnp.float32))
        top_w, sel = jax.lax.top_k(router_probs, TOP_K)
        top_w = top_w / (top_w.sum(axis=-1, keepdims=True) + 1e-20)
        top_w = top_w.astype(x.dtype)
        W1e = w1.reshape(D, E, W).transpose(1, 0, 2)
        W2e = w2.reshape(E, W, D)
        h = jnp.einsum('td,edw->etw', xf, W1e)
        a = jnp.square(jax.nn.relu(h))
        y = jnp.einsum('etw,ewd->etd', a, W2e)
        cw = jnp.zeros((T, E), dtype=x.dtype).at[jnp.arange(T)[:, None], sel].set(top_w)
        out = jnp.einsum('etd,te->td', y, cw)
        return out.reshape(B, S, D)

    def _L1_attn_ref(x, Wq, bq, Wk, bk, Wv, bv, gamma, beta):
        import jax, jax.numpy as jnp
        import numpy as np
        DIM = 128
        H = 16
        HD = DIM // H
        EPS_DENOM = 1e-06
        EPS_LN = 1e-05
        B, N, C = x.shape
        q = (x @ Wq.T + bq).reshape(B, N, H, HD)
        k = (x @ Wk.T + bk).reshape(B, N, H, HD)
        v = (x @ Wv.T + bv).reshape(B, N, H, HD)
        q = jax.nn.relu(q)
        k = jax.nn.relu(k)
        kv = jnp.einsum('bnhd,bnhp->bhdp', k, v)
        k_sum = k.sum(axis=1)
        denom = jnp.einsum('bnhd,bhd->bnh', q, k_sum)
        denom = jnp.maximum(denom, EPS_DENOM)[..., None]
        ctx = jnp.einsum('bnhd,bhdp->bnhp', q, kv)
        out = (ctx / denom).reshape(B, N, C)
        y = out + x
        mu = y.mean(axis=-1, keepdims=True)
        var = y.var(axis=-1, keepdims=True)
        return (y - mu) / jnp.sqrt(var + EPS_LN) * gamma + beta

    def _L1_ffn_ref(x, W_r, W_k, W_v, mu_r, mu_k):
        import jax, jax.numpy as jnp
        import numpy as np
        DIM = 128

        def _reference_tuple_inner(x, W_r, W_k, W_v, mu_r, mu_k):
            B, T, C = x.shape
            x_prev = jnp.concatenate([jnp.zeros((B, 1, C), x.dtype), x[:, :-1, :]], axis=1)
            xr = mu_r * x + (1.0 - mu_r) * x_prev
            xk = mu_k * x + (1.0 - mu_k) * x_prev
            r = jax.nn.sigmoid(jnp.einsum('btc,dc->btd', xr, W_r))
            k = jnp.einsum('btc,dc->btd', xk, W_k)
            k_act = jnp.square(jax.nn.relu(k))
            out = r * jnp.einsum('btc,dc->btd', k_act, W_v)
            new_state = x[:, -1, :]
            return (out, new_state)
        return _reference_tuple_inner(x, W_r, W_k, W_v, mu_r, mu_k)[0]
    x = L0_attn_x
    xn = _layernorm(x, axis=-1)
    s = _L0_attn_ref(xn, L0_attn_ln_g, L0_attn_ln_b, L0_attn_Wx, L0_attn_Ww, L0_attn_bw, L0_attn_Wk, L0_attn_Wv, L0_attn_Wr, L0_attn_Wo)
    g = _silu(_L0_ffn_ref(xn, L0_ffn_router_w, L0_ffn_w1, L0_ffn_w2))
    x = x + s * g
    xn = _layernorm(x, axis=-1)
    s = _L1_attn_ref(xn, L1_attn_Wq, L1_attn_bq, L1_attn_Wk, L1_attn_bk, L1_attn_Wv, L1_attn_bv, L1_attn_gamma, L1_attn_beta)
    g = _silu(_L1_ffn_ref(xn, L1_ffn_W_r, L1_ffn_W_k, L1_ffn_W_v, L1_ffn_mu_r, L1_ffn_mu_k))
    x = x + s * g
    return x

_drawn_inputs = setup_inputs


def setup_inputs(seed=0):
    import zlib

    import numpy as np

    out = dict(_drawn_inputs(seed))
    spreads = {'L0_attn_ln_g': (1.0, 0.6),
     'L0_attn_ln_b': (0.0, 0.8),
     'L0_attn_bw': (0.0, 0.8),
     'L1_attn_bq': (0.0, 0.8),
     'L1_attn_bk': (0.0, 0.8),
     'L1_attn_bv': (0.0, 0.8),
     'L1_attn_gamma': (1.0, 0.6),
     'L1_attn_beta': (0.0, 0.8)}
    factors = {'L0_attn_Wx': 8.0,
     'L0_attn_Ww': 8.0,
     'L0_attn_Wr': 5.067,
     'L1_attn_Wq': 8.0,
     'L1_attn_Wk': 8.0,
     'L1_attn_Wv': 8.0,
     'L1_ffn_W_r': 5.855,
     'L1_ffn_mu_r': 8.0}
    for name, (base, spread) in spreads.items():
        noise = np.random.default_rng([zlib.crc32(name.encode()), seed]).standard_normal(out[name].shape)
        drawn = base * np.exp(spread * noise) if base else spread * noise
        out[name] = jnp.asarray(drawn.astype(out[name].dtype))
    for name, factor in factors.items():
        out[name] = (out[name] * factor).astype(out[name].dtype)
    return out
```

```python
from contextlib import ExitStack

import numpy as np

import concourse.bass as bass
from concourse import mybir

ALU = mybir.AluOpType
ACT = mybir.ActivationFunctionType
F32 = mybir.dt.float32
U32 = mybir.dt.uint32

P = 128
B, T = 32, 256
TILES = 4
G = TILES * P
SEQ = G // T
CH = T // P
LANES = 2
TURNS = B * T // (LANES * G)
NH, HS = 2, 64
LEVELS = 7
E, W = 8, 128
AH, AD = 16, 8
EPS = 1e-5
EPS_DENOM = 1e-6

FILLS = {
    "c0": ["xnT", "decay", "r", "vw_hi", "level0", "level2", "level4", "level6", "y",
           "xn1T", "kv_hi", "ctx_lo"],
    "c1": ["znT", "k", "vw_lo", "route_diag", "level1", "level3", "level5", "level7",
           "kv_lo", "kvm"],
    "h": [f"h{e}" for e in range(E)] + ["q", "ffn_r", "ctx_hi"],
    "y": [f"y{e}" for e in range(E)] + ["ffn_k", "ffn_v"],
}
WHERE = {name: (bank, n + 1) for bank, names in FILLS.items() for n, name in enumerate(names)}

COLUMNS = ["ln_g", "ln_b", "bw", "bq", "mu_r", "mu_k"]
ROWS = ["bkv", "gamma", "beta"]


def build(nc, x, w, out):
    x_tiles = x.rearrange("b (c p) d -> p (b c) d", p=P)
    out_tiles = out.rearrange("b (c p) d -> p (b c) d", p=P)

    with ExitStack() as ctx:
        def sb(name, shape, dt=F32):
            return ctx.enter_context(nc.sbuf_tensor(name, shape, dt))

        def lanes(name, shape, dt=F32):
            return [sb(f"{name}{g}", shape, dt) for g in range(LANES)]

        def sem(name):
            return ctx.enter_context(nc.semaphore(name))

        def sems(name):
            return [sem(f"{name}{g}") for g in range(LANES)]

        WT = {n: sb("w_" + n, list(w[n].shape)) for n in w if n not in COLUMNS + ROWS}
        COL = {n: sb("c_" + n, [P, 1]) for n in COLUMNS}
        ROW = {n: sb("r_" + n, [P, w[n].shape[1]]) for n in ROWS}
        neg_bw = sb("neg_bw", [P, 1])
        w_decay = sb("w_decay", [P, P])
        w_vo = sb("w_vo", [P, NH * P])
        minus_half = sb("minus_half", [P, TILES])

        x_in = lanes("x_in", [P, TILES, P])
        stats = lanes("stats", [P, TILES, 6])
        mv = lanes("mv", [P, TILES, 2])
        ln_t = lanes("ln_t", [P, 6, TILES])
        xn = lanes("xn", [P, TILES, P])
        zn = lanes("zn", [P, TILES, P])
        xnT = lanes("xnT", [P, G])
        znT = lanes("znT", [P, G])
        decay = lanes("decay", [P, G])
        r_sig = lanes("r_sig", [P, G])
        kF = lanes("kF", [P, G])
        rF = lanes("rF", [P, NH, G])
        rk = lanes("rk", [P, G])
        tot = [lanes(f"tot{l}_", [P, G >> l]) for l in range(1, LEVELS)]
        a_diag = lanes("a_diag", [P, TILES, NH, P])
        a_off = lanes("a_off", [P, SEQ, NH, P])
        vw = lanes("vw", [P, TILES, NH * P])
        probs = lanes("probs", [P, TILES, 16])
        top = lanes("top", [P, TILES, E])
        pick = lanes("pick", [P, TILES, E])
        rest = lanes("rest", [P, TILES, 16])
        den = lanes("den", [P, TILES])
        cw = lanes("cw", [P, TILES, E])
        u = lanes("u", [P, G])
        act_sq = lanes("act_sq", [P, G])
        moe = lanes("moe", [P, TILES, P])
        sig0 = lanes("sig0", [P, TILES, P])
        gate0 = lanes("gate0", [P, TILES, P])
        x1 = lanes("x1", [P, TILES, P])
        xn1 = lanes("xn1", [P, TILES, P])
        xn1T = lanes("xn1T", [P, SEQ, T + 1])
        diff = lanes("diff", [P, SEQ, T])
        xr = lanes("xr", [P, SEQ, T])
        xk = lanes("xk", [P, SEQ, T])
        qT = lanes("qT", [P, G])
        k_pre = lanes("k_pre", [P, TILES, P])
        k_tok = lanes("k_tok", [P, TILES, P])
        v_tok = lanes("v_tok", [P, TILES, P + 1])
        kvm = lanes("kvm", [P, SEQ, P + AH])
        rden = lanes("rden", [P, TILES, AH])
        dmax = lanes("dmax", [P, TILES, AH])
        att = lanes("att", [P, TILES, P])
        ysum = lanes("ysum", [P, TILES, P])
        s2 = lanes("s2", [P, TILES, P])
        r2 = lanes("r2", [P, TILES, P])
        ku = lanes("ku", [P, G])
        ksq = lanes("ksq", [P, G])
        f2 = lanes("f2", [P, TILES, P])
        sig1 = lanes("sig1", [P, TILES, P])
        o_out = lanes("o_out", [P, TILES, P])

        bank = {b: [ctx.enter_context(nc.psum_tensor(f"bank_{b}{g}", [P, 512], F32))
                    for g in range(LANES)] for b in FILLS}
        filled = {b: sems(f"filled_{b}") for b in FILLS}
        free = {b: sems(f"free_{b}") for b in FILLS}

        loaded = sem("loaded")
        prep_mm = sem("prep_mm")
        prep_done = sem("prep_done")
        memset_done = sem("memset_done")
        x_loaded = sems("x_loaded")
        x_free = sems("x_free")
        stored = sems("stored")
        dve_step = sem("dve_step")
        pool_step = sem("pool_step")
        passed = {nc.vector.engine: sem("dve_passed"), nc.gpsimd.engine: sem("pool_passed")}
        names = ["act_sq", "cw", "gate0", "gate1", "kF_level", "k_pre", "k_tok", "ksq", "mv0", "mv1", "mv2", "out", "probs", "rF0", "rF_level", "rk", "rstd0", "rstd1", "rstd2", "s2", "sig0", "sig1", "tot_level", "xk", "xn", "xn1", "xr", "zn"]
        done = {n: sems(n + "_done") for n in names}

        block = ctx.enter_context(nc.Block())

        def full(eng, i, g, name):
            b, k = WHERE[name]
            eng.wait_ge(filled[b][g], i * len(FILLS[b]) + k)

        def writable(eng, i, g, name):
            b, k = WHERE[name]
            eng.wait_ge(free[b][g], i * len(FILLS[b]) + k)

        def drained(eng, i, g, name):
            b, k = WHERE[name]
            eng.wait_ge(free[b][g], i * len(FILLS[b]) + k + 1)

        def stand_alone(eng):
            eng.sem_inc(passed[eng.engine], 1)

        def fills(ins, g, name):
            ins.then_inc(filled[WHERE[name][0]][g], 1)

        def drains(ins, g, name):
            ins.then_inc(free[WHERE[name][0]][g], 1)

        def at(name, g):
            return bank[WHERE[name][0]][g]

        def ready(eng, i, g, name, k=1, per=1):
            eng.wait_ge(done[name][g], i * per + k)

        n_loads = len(w)

        @block.sync
        def _(sp):
            for n in w:
                dst = COL[n][:] if n in COLUMNS else ROW[n][:] if n in ROWS else WT[n][:]
                src = w[n].to_broadcast([P, w[n].shape[1]]) if n in ROWS else w[n]
                sp.dma_start(dst, src).then_inc(loaded, 16)
            with sp.Fori(0, TURNS) as i:
                for g in range(LANES):
                    sp.wait_ge(x_free[g], i + 1)
                    sp.dma_start(x_in[g][:], x_tiles[:, bass.ds(i * (LANES * TILES) + g * TILES, TILES), :]
                                 ).then_inc(x_loaded[g], 16)

        @block.tensor
        def _(pe):
            mm = nc.tensor.matmul
            pe.wait_ge(loaded, 16 * n_loads)
            mm(bank["c0"][0][:, 0:P], WT["WxT"][:], WT["Ww"][:], start=True, stop=True)
            for h in range(NH):
                rows = slice(h * HS, (h + 1) * HS)
                last = mm(bank["h" if h else "c1"][0][:, 0:P], WT["WvT0"][rows, :], WT["Wo"][rows, :],
                          start=True, stop=True)
            last.then_inc(prep_mm, 1)
            pe.wait_ge(prep_done, 4)
            pe.wait_ge(memset_done, 1)

            def transposes(i, g, name, src):
                writable(pe, i, g, name)
                for j in range(TILES):
                    last = nc.tensor.transpose(at(name, g)[:, j * P:(j + 1) * P], src[:, j, :], WT["ident"][:])
                fills(last, g, name)

            def product(i, g, name, weight, moving):
                writable(pe, i, g, name)
                fills(mm(at(name, g)[:], weight, moving, start=True, stop=True), g, name)

            def token_product(i, g, name, tokT, weight, tiles, step):
                writable(pe, i, g, name)
                n = weight.shape[1]
                for m, j in enumerate(tiles):
                    last = mm(at(name, g)[:, m * step:m * step + n], tokT[:, j * P:(j + 1) * P], weight,
                              start=True, stop=True)
                fills(last, g, name)

            def route_diag(i, g):
                writable(pe, i, g, "route_diag")
                ps = at("route_diag", g)
                for j in range(TILES):
                    mm(ps[:, j * E:(j + 1) * E], xnT[g][:, j * P:(j + 1) * P], WT["routerT"][:],
                       start=True, stop=True)
                ready(pe, i, g, "rk")
                for j in range(TILES):
                    last = mm(ps[:, 64 + j * NH:64 + (j + 1) * NH], rk[g][:, j * P:(j + 1) * P],
                              WT["head_cols"][:], start=True, stop=True)
                fills(last, g, "route_diag")

            def level(i, g, l):
                name = f"level{l}"
                if l == 0:
                    drained(pe, i, g, "k")
                    ready(pe, i, g, "rF0")
                else:
                    ready(pe, i, g, "kF_level", l, LEVELS)
                    ready(pe, i, g, "rF_level", l, LEVELS)
                writable(pe, i, g, name)
                ps = at(name, g)
                if l < LEVELS:
                    half = 1 << l
                    for j in range(TILES):
                        q = rF[g][:, :, j * P:(j + 1) * P].rearrange("p h (n two k) -> p h n two k",
                                                                     two=2, k=half)[:, :, :, 1, :]
                        last = mm(ps[:, j * P:(j + 1) * P], kF[g][:, j * P:(j + 1) * P], q,
                                  start=True, stop=True)
                else:
                    for s in range(SEQ):
                        j = s * CH
                        last = mm(ps[:, s * NH * P:(s + 1) * NH * P], kF[g][:, j * P:(j + 1) * P],
                                  rF[g][:, :, (j + 1) * P:(j + 2) * P], start=True, stop=True)
                fills(last, g, name)

            def expert_in(i, g, e):
                product(i, g, f"h{e}", WT["w1"][:, e * W:(e + 1) * W], xnT[g][:])

            def expert_out(i, g, e):
                name = f"y{e}"
                writable(pe, i, g, name)
                ready(pe, i, g, "act_sq", e + 1, E)
                for j in range(TILES):
                    last = mm(at(name, g)[:, j * P:(j + 1) * P], act_sq[g][:, j * P:(j + 1) * P],
                              WT["w2"][:, e, :], start=True, stop=True)
                fills(last, g, name)

            def mix(i, g):
                writable(pe, i, g, "y")
                drained(pe, i, g, "level7")
                for j in range(TILES):
                    o = at("y", g)[:, j * P:(j + 1) * P]
                    parts = [(a_diag[g][:, j, h, :], vw[g][:, j, h * P:(h + 1) * P]) for h in range(NH)]
                    if j % CH:
                        parts += [(a_off[g][:, j // CH, h, :], vw[g][:, j - 1, h * P:(h + 1) * P])
                                  for h in range(NH)]
                    for n, (s, v) in enumerate(parts):
                        last = mm(o, s, v, start=(n == 0), stop=(n == len(parts) - 1))
                fills(last, g, "y")

            def kv_sums(i, g):
                writable(pe, i, g, "kvm")
                ready(pe, i, g, "k_tok", 2, 2)
                drained(pe, i, g, "kv_hi")
                for s in range(SEQ):
                    for c in range(CH):
                        j = s * CH + c
                        last = mm(at("kvm", g)[:, s * 256:s * 256 + P + 1], k_tok[g][:, j, :],
                                  v_tok[g][:, j, :], start=(c == 0), stop=(c == CH - 1))
                fills(last, g, "kvm")

            def context(i, g, name, tiles):
                writable(pe, i, g, name)
                drained(pe, i, g, "q")
                drained(pe, i, g, "kvm")
                for m, j in enumerate(tiles):
                    last = mm(at(name, g)[:, m * 256:m * 256 + P + AH], qT[g][:, j * P:(j + 1) * P],
                              kvm[g][:, j // CH, :], start=True, stop=True)
                fills(last, g, name)

            both = range(LANES)
            with pe.Fori(0, TURNS) as i:
                for g in both:
                    ready(pe, i, g, "xn")
                    transposes(i, g, "xnT", xn[g])
                    ready(pe, i, g, "zn")
                    transposes(i, g, "znT", zn[g])
                for g in both:
                    drained(pe, i, g, "znT")
                    product(i, g, "decay", w_decay[:], znT[g][:])
                    product(i, g, "k", WT["Wk0"][:], znT[g][:])
                for g in both:
                    product(i, g, "r", WT["Wr0"][:], znT[g][:])
                for g in both:
                    drained(pe, i, g, "xnT")
                    expert_in(i, g, 0)
                for g in both:
                    token_product(i, g, "vw_lo", znT[g], w_vo[:], range(0, 2), NH * P)
                    token_product(i, g, "vw_hi", znT[g], w_vo[:], range(2, 4), NH * P)
                for g in both:
                    route_diag(i, g)
                for n in range(E):
                    for g in both:
                        level(i, g, n)
                    for g in both:
                        expert_out(i, g, n)
                    if n + 1 < E:
                        for g in both:
                            expert_in(i, g, n + 1)
                for g in both:
                    mix(i, g)
                for g in both:
                    ready(pe, i, g, "xn1")
                    transposes(i, g, "xn1T", xn1[g])
                for g in both:
                    drained(pe, i, g, "xn1T")
                    writable(pe, i, g, "q")
                    fills(mm(at("q", g)[:], WT["WqT"][:], xn1T[g][:, :, 1:], start=True, stop=True), g, "q")
                    for name, tiles in (("kv_lo", (0, 1)), ("kv_hi", (2, 3))):
                        writable(pe, i, g, name)
                        for m, j in enumerate(tiles):
                            c = 1 + (j % CH) * P
                            last = mm(at(name, g)[:, m * 256:(m + 1) * 256], xn1T[g][:, j // CH, c:c + P],
                                      WT["WkvT"][:], start=True, stop=True)
                        fills(last, g, name)
                for g in both:
                    ready(pe, i, g, "xk")
                    product(i, g, "ffn_k", WT["fWkT"][:], xk[g][:].rearrange("p s t -> p (s t)"))
                    ready(pe, i, g, "xr")
                    token_product(i, g, "ffn_r", xr[g][:].rearrange("p s t -> p (s t)"), WT["fWrT"][:],
                                  range(TILES), P)
                for g in both:
                    kv_sums(i, g)
                for g in both:
                    ready(pe, i, g, "ksq")
                    token_product(i, g, "ffn_v", ksq[g], WT["fWvT"][:], range(TILES), P)
                for g in both:
                    context(i, g, "ctx_lo", (0, 1))
                    context(i, g, "ctx_hi", (2, 3))

        @block.scalar
        def _(act):
            af = nc.scalar.activation
            act.wait_ge(loaded, 16 * n_loads)
            nc.scalar.mul(neg_bw[:], COL["bw"][:], -1.0).then_inc(prep_done, 1)
            act.wait_ge(prep_mm, 1)
            nc.scalar.copy(w_decay[:], bank["c0"][0][:, 0:P]).then_inc(prep_done, 1)
            nc.scalar.copy(w_vo[:, 0:P], bank["c1"][0][:, 0:P]).then_inc(prep_done, 1)
            nc.scalar.copy(w_vo[:, P:2 * P], bank["h"][0][:, 0:P]).then_inc(prep_done, 1)
            act.wait_ge(prep_done, 4)
            act.wait_ge(memset_done, 1)

            def drain(i, g, name, o, func, **kw):
                full(act, i, g, name)
                drains(af(o, at(name, g)[:], func, **kw), g, name)

            def expert_act(i, g, e):
                drain(i, g, f"h{e}", u[g][:], ACT.Relu)
                drained(act, i, g, f"h{e}")
                if e:
                    b, k = WHERE[f"y{e - 1}"]
                    act.wait_ge(filled[b][g], i * len(FILLS[b]) + k)
                af(act_sq[g][:], u[g][:], ACT.Square).then_inc(done["act_sq"][g], 1)

            both = range(LANES)
            with act.Fori(0, TURNS) as i:
                for g in both:
                    drain(i, g, "xnT", xnT[g][:], ACT.Copy)
                    drain(i, g, "znT", znT[g][:], ACT.Identity,
                          bias=COL["ln_b"][:], scale=COL["ln_g"][:])
                for g in both:
                    drain(i, g, "decay", decay[g][:], ACT.Sigmoid,
                          bias=neg_bw[:], scale=-1.0)
                    drain(i, g, "k", kF[g][:], ACT.Copy)
                for g in both:
                    drain(i, g, "r", r_sig[g][:], ACT.Sigmoid)
                for g in both:
                    expert_act(i, g, 0)
                for g in both:
                    drain(i, g, "vw_lo", vw[g][:, 0:2, :].rearrange("p j n -> p (j n)"),
                          ACT.Copy)
                    drain(i, g, "vw_hi", vw[g][:, 2:4, :].rearrange("p j n -> p (j n)"),
                          ACT.Copy)
                for g in both:
                    full(act, i, g, "route_diag")
                    af(probs[g][:, :, 0:E], at("route_diag", g)[:, 0:TILES * E].rearrange(
                        "p (j e) -> p j e", e=E), ACT.Sigmoid).then_inc(done["probs"][g], 1)
                for e in range(1, E):
                    for g in both:
                        expert_act(i, g, e)
                for g in both:
                    drain(i, g, "level7", a_off[g][:].rearrange("p s h t -> p (s h t)"),
                          ACT.Copy)
                for g in both:
                    drained(act, i, g, f"y{E - 1}")
                    af(sig0[g][:], moe[g][:], ACT.Sigmoid).then_inc(done["sig0"][g], 1)
                for g in both:
                    full(act, i, g, "xn1T")
                    for s in range(SEQ):
                        ins = af(xn1T[g][:, s, 1:], at("xn1T", g)[:, s * T:(s + 1) * T], ACT.Copy)
                    drains(ins, g, "xn1T")
                for g in both:
                    drain(i, g, "q", qT[g][:], ACT.Relu, bias=COL["bq"][:])
                    for m in range(2):
                        ready(act, i, g, "k_pre", m + 1, 2)
                        af(k_tok[g][:, 2 * m:2 * m + 2, :], k_pre[g][:, 2 * m:2 * m + 2, :], ACT.Relu
                           ).then_inc(done["k_tok"][g], 1)
                for g in both:
                    drain(i, g, "ffn_k", ku[g][:], ACT.Relu)
                    drained(act, i, g, "ffn_k")
                    af(ksq[g][:], ku[g][:], ACT.Square).then_inc(done["ksq"][g], 1)
                    drain(i, g, "ffn_r", r2[g][:].rearrange("p j n -> p (j n)"),
                          ACT.Sigmoid)
                for g in both:
                    drained(act, i, g, "ffn_v")
                    af(sig1[g][:], f2[g][:], ACT.Sigmoid).then_inc(done["sig1"][g], 1)
                for g in both:
                    ready(act, i, g, "out")
                    act.dma_start(out_tiles[:, bass.ds(i * (LANES * TILES) + g * TILES, TILES), :],
                                  o_out[g][:]).then_inc(stored[g], 16)
            for g in both:
                act.wait_ge(stored[g], 16 * TURNS + 16)

        DVE_STEPS = LANES * 14
        POOL_STEPS = LANES * 10

        @block.vector
        def _(dve):
            tt, ts, stt = nc.vector.tensor_tensor, nc.vector.tensor_scalar, nc.vector.scalar_tensor_tensor
            for g in range(LANES):
                nc.vector.memset(rF[g][:], 0.0)
                nc.vector.memset(a_diag[g][:], 0.0)
                nc.vector.memset(xn1T[g][:], 0.0)
                nc.vector.memset(v_tok[g][:], 1.0)
                nc.vector.memset(probs[g][:], -1.0)
                nc.vector.memset(pick[g][:], -1.0)
            nc.vector.memset(minus_half[:], -0.5).then_inc(memset_done, 1)
            dve.wait_ge(memset_done, 1)
            dve.wait_ge(loaded, 16 * n_loads)
            dve.wait_ge(prep_done, 4)
            for g in range(LANES):
                for b in FILLS:
                    dve.sem_inc(free[b][g], 1)
                dve.sem_inc(x_free[g], 1)
                dve.sem_inc(stored[g], 16)
            steps = [0]

            def step(i, ins):
                steps[0] += 1
                ins.then_inc(dve_step, 1)
                dve.wait_ge(dve_step, i * DVE_STEPS + steps[0])

            def moments(i, g, src, name):
                for j in range(TILES):
                    last = nc.vector.bn_stats(stats[g][:, j, :], src[:, j, :])
                step(i, last)
                stand_alone(dve)
                for j in range(TILES):
                    last = nc.vector.bn_aggr(mv[g][:, j, :], stats[g][:, j, :])
                last.then_inc(done[name][g], 1)

            def normalise(i, g, o, src, mean, scale, name):
                for j in range(TILES):
                    last = ts(o[:, j, :], src[:, j, :], mean[:, j:j + 1], scale[:, j:j + 1],
                              ALU.subtract, ALU.mult)
                last.then_inc(done[name][g], 1)

            def level_scores(i, g, l):
                half = 1 << l
                full(dve, i, g, f"level{l}")
                drained(dve, i, g, f"level{l - 1}" if l else "route_diag")
                o = a_diag[g][:].rearrange("p j h (n two k) -> p (j h) n two k", two=2, k=half)[:, :, :, 1, :]
                ps = at(f"level{l}", g)[:].rearrange("p (m n k) -> p m n k", m=TILES * NH, k=half)
                m = WT["level_mask"][:, l * HS:(l + 1) * HS].bitcast(U32).rearrange(
                    "p (n k) -> p n k", k=half).unsqueeze(1).to_broadcast([P, TILES * NH, HS // half, half])
                stand_alone(dve)
                ins = nc.vector.copy_predicated(o, m, ps)
                drains(ins, g, f"level{l}")

            def grow_r(i, g, l):
                half = 1 << l
                full(dve, i, g, f"level{l}")
                if l:
                    ready(dve, i, g, "tot_level", l, LEVELS - 1)
                    dve.wait_ge(done["rF_level"][g], i * LEVELS + l)
                t = decay[g] if l == 0 else tot[l - 1][g]
                right = rF[g][:].rearrange("p h (n two k) -> p h n two k", two=2, k=half)[:, :, :, 1, :]
                left_tot = t[:].rearrange("p (n two) -> p n two", two=2)[:, :, 0:1]
                left_tot = left_tot.unsqueeze(1).to_broadcast([P, NH, G // (2 * half), half])
                tt(right, right, left_tot, ALU.mult).then_inc(done["rF_level"][g], 1)

            def weigh(i, g, e):
                full(dve, i, g, f"y{e}")
                if e:
                    drained(dve, i, g, f"y{e - 1}")
                for j in range(TILES):
                    ps = at(f"y{e}", g)[:, j * P:(j + 1) * P]
                    c = cw[g][:, j, e:e + 1]
                    if e == 0:
                        ins = ts(moe[g][:, j, :], ps, c, None, ALU.mult)
                    else:
                        ins = stt(moe[g][:, j, :], ps, c, moe[g][:, j, :], ALU.mult, ALU.add)
                drains(ins, g, f"y{e}")

            def route(i, g):
                ready(dve, i, g, "probs")
                stand_alone(dve)
                for j in range(TILES):
                    last = nc.vector.max(top[g][:, j, :], probs[g][:, j, 0:E])
                step(i, last)
                nc.vector.tensor_copy(pick[g][:, :, 0:2], top[g][:, :, 0:2])
                step(i, tt(den[g][:], top[g][:, :, 0], top[g][:, :, 1], ALU.add))
                ts(den[g][:], den[g][:], 1e-20, None, ALU.add)
                for j in range(TILES):
                    last = nc.vector.match_replace(rest[g][:, j, :], pick[g][:, j, :], probs[g][:, j, :], 0.0)
                step(i, last)
                nc.vector.reciprocal(den[g][:], den[g][:])
                step(i, tt(cw[g][:], probs[g][:, :, 0:E], rest[g][:, :, 0:E], ALU.subtract))
                tt(cw[g][:], cw[g][:], den[g][:].unsqueeze(2).to_broadcast([P, TILES, E]), ALU.mult
                   ).then_inc(done["cw"][g], 1)
                ready(dve, i, g, "cw")

            both = range(LANES)
            with dve.Fori(0, TURNS) as i:
                steps[0] = 0
                for g in both:
                    dve.wait_ge(x_loaded[g], 16 * i + 16)
                    moments(i, g, x_in[g], "mv0")
                for g in both:
                    ready(dve, i, g, "rstd0")
                    normalise(i, g, xn[g], x_in[g], mv[g][:, :, 0], ln_t[g][:, 0, :], "xn")
                    normalise(i, g, zn[g], x_in[g], mv[g][:, :, 0], ln_t[g][:, 1, :], "zn")
                for g in both:
                    drained(dve, i, g, "r")
                    drained(dve, i, g, "decay")
                    for h in range(NH):
                        rows = slice(h * HS, (h + 1) * HS)
                        last = tt(rF[g][rows, h, :], r_sig[g][rows, :], decay[g][rows, :], ALU.mult)
                    last.then_inc(done["rF0"][g], 1)
                for g in both:
                    full(dve, i, g, "route_diag")
                    ready(dve, i, g, "probs")
                    d = at("route_diag", g)[:, 64:64 + TILES * NH].unsqueeze(2).to_broadcast([P, TILES * NH, P])
                    m = WT["ident"][:].bitcast(U32).unsqueeze(1).to_broadcast([P, TILES * NH, P])
                    stand_alone(dve)
                    ins = nc.vector.copy_predicated(a_diag[g][:].rearrange("p j h t -> p (j h) t"), m, d)
                    drains(ins, g, "route_diag")
                for n in range(E):
                    for g in both:
                        if n < LEVELS:
                            if n == 0:
                                ready(dve, i, g, "rF0")
                            grow_r(i, g, n)
                            level_scores(i, g, n)
                    if n == 0:
                        for g in both:
                            route(i, g)
                    for g in both:
                        weigh(i, g, n)
                for g in both:
                    ready(dve, i, g, "gate0")
                    full(dve, i, g, "y")
                    ins = tt(x1[g][:].rearrange("p j n -> p (j n)"), at("y", g)[:],
                             gate0[g][:].rearrange("p j n -> p (j n)"), ALU.mult)
                    drains(ins, g, "y")
                    drained(dve, i, g, "y")
                    tt(x1[g][:], x1[g][:], x_in[g][:], ALU.add).then_inc(x_free[g], 1)
                    dve.wait_ge(x_free[g], i + 2)
                    moments(i, g, x1[g], "mv1")
                for g in both:
                    ready(dve, i, g, "rstd1")
                    normalise(i, g, xn1[g], x1[g], mv[g][:, :, 0], ln_t[g][:, 0, :], "xn1")
                for g in both:
                    drained(dve, i, g, "xn1T")
                    prev = xn1T[g][:, :, 0:T]
                    step(i, tt(diff[g][:], xn1T[g][:, :, 1:], prev, ALU.subtract))
                    stt(xk[g][:], diff[g][:], COL["mu_k"][:], prev, ALU.mult, ALU.add
                        ).then_inc(done["xk"][g], 1)
                    stt(xr[g][:], diff[g][:], COL["mu_r"][:], prev, ALU.mult, ALU.add
                        ).then_inc(done["xr"][g], 1)
                    for m, name in enumerate(("kv_lo", "kv_hi")):
                        full(dve, i, g, name)
                        ps = at(name, g)[:].rearrange("p (j n) -> p j n", n=2 * P)
                        js = slice(2 * m, 2 * m + 2)
                        tt(k_pre[g][:, js, :], ps[:, :, 0:P],
                           ROW["bkv"][:, 0:P].unsqueeze(1).to_broadcast([P, 2, P]), ALU.add
                           ).then_inc(done["k_pre"][g], 1)
                        ins = tt(v_tok[g][:, js, 0:P], ps[:, :, P:2 * P],
                                 ROW["bkv"][:, P:2 * P].unsqueeze(1).to_broadcast([P, 2, P]), ALU.add)
                        drains(ins, g, name)
                for g in both:
                    full(dve, i, g, "kvm")
                    ps = at("kvm", g)[:].rearrange("p (s n) -> p s n", n=256)
                    tt(kvm[g][:, :, 0:P], ps[:, :, 0:P],
                       WT["block_mask"][:].unsqueeze(1).to_broadcast([P, SEQ, P]), ALU.mult)
                    ins = tt(kvm[g][:, :, P:], ps[:, :, P:P + 1].to_broadcast([P, SEQ, AH]),
                             WT["head_mask"][:].unsqueeze(1).to_broadcast([P, SEQ, AH]), ALU.mult)
                    drains(ins, g, "kvm")
                for g in both:
                    full(dve, i, g, "ffn_v")
                    drained(dve, i, g, "ffn_r")
                    ins = tt(f2[g][:].rearrange("p j n -> p (j n)"), at("ffn_v", g)[:],
                             r2[g][:].rearrange("p j n -> p (j n)"), ALU.mult)
                    drains(ins, g, "ffn_v")
                for g in both:
                    for m, name in enumerate(("ctx_lo", "ctx_hi")):
                        js = slice(2 * m, 2 * m + 2)
                        full(dve, i, g, name)
                        ps = at(name, g)[:].rearrange("p (j n) -> p j n", n=256)
                        step(i, ts(dmax[g][:, js, :], ps[:, :, P:P + AH], EPS_DENOM, None, ALU.max))
                        step(i, nc.vector.reciprocal(rden[g][:, js, :], dmax[g][:, js, :]))
                        ins = tt(att[g][:, js, :].rearrange("p j (h d) -> p j h d", d=AD),
                                 ps[:, :, 0:P].rearrange("p j (h d) -> p j h d", d=AD),
                                 rden[g][:, js, :].unsqueeze(3).to_broadcast([P, 2, AH, AD]), ALU.mult)
                        drains(ins, g, name)
                    drained(dve, i, g, "ctx_lo")
                    drained(dve, i, g, "ctx_hi")
                    step(i, tt(ysum[g][:], att[g][:], xn1[g][:], ALU.add))
                    moments(i, g, ysum[g], "mv2")
                for g in both:
                    ready(dve, i, g, "rstd2")
                    normalise(i, g, s2[g], ysum[g], mv[g][:, :, 0], ln_t[g][:, 0, :], "s2")
                for g in both:
                    ready(dve, i, g, "s2")
                    step(i, tt(s2[g][:], s2[g][:], ROW["gamma"][:].unsqueeze(1).to_broadcast([P, TILES, P]),
                               ALU.mult))
                    tt(s2[g][:], s2[g][:], ROW["beta"][:].unsqueeze(1).to_broadcast([P, TILES, P]), ALU.add
                       ).then_inc(done["gate1"][g], 1)
            assert steps[0] == DVE_STEPS, steps[0]

        @block.gpsimd
        def _(pool):
            tt, ts = nc.gpsimd.tensor_tensor, nc.gpsimd.tensor_scalar
            pool.wait_ge(memset_done, 1)
            steps = [0]

            def step(i, ins):
                steps[0] += 1
                ins.then_inc(pool_step, 1)
                pool.wait_ge(pool_step, i * POOL_STEPS + steps[0])

            def rstd(i, g, name, twice=False):
                t = ln_t[g]
                var = mv[g][:, :, 1]
                stand_alone(pool)
                step(i, ts(t[:, 2, :], var, EPS, 1.0, ALU.add, ALU.mult))
                ins = tt(t[:, 0, :], t[:, 2, :], minus_half[:], ALU.pow)
                if not twice:
                    ins.then_inc(done[name][g], 1)
                    return
                step(i, ins)
                step(i, tt(t[:, 3, :], var, t[:, 0, :], ALU.mult))
                step(i, tt(t[:, 3, :], t[:, 3, :], t[:, 0, :], ALU.mult))
                stand_alone(pool)
                step(i, ts(t[:, 3, :], t[:, 3, :], EPS, 1.0, ALU.add, ALU.mult))
                step(i, tt(t[:, 4, :], t[:, 3, :], minus_half[:], ALU.pow))
                tt(t[:, 1, :], t[:, 0, :], t[:, 4, :], ALU.mult).then_inc(done[name][g], 1)

            def grow_k(i, g, l):
                half = 1 << l
                t = decay[g] if l == 0 else tot[l - 1][g]
                pair = t[:].rearrange("p (n two) -> p n two", two=2)
                if l < LEVELS - 1:
                    if l:
                        ready(pool, i, g, "tot_level", l, LEVELS - 1)
                    tt(tot[l][g][:], pair[:, :, 0], pair[:, :, 1], ALU.mult).then_inc(done["tot_level"][g], 1)
                else:
                    ready(pool, i, g, "tot_level", l, LEVELS - 1)
                full(pool, i, g, f"level{l}")
                if l:
                    ready(pool, i, g, "kF_level", l, LEVELS)
                left = kF[g][:].rearrange("p (n two k) -> p n two k", two=2, k=half)[:, :, 0, :]
                tt(left, left, pair[:, :, 1:2].to_broadcast([P, G // (2 * half), half]), ALU.mult
                   ).then_inc(done["kF_level"][g], 1)

            both = range(LANES)
            with pool.Fori(0, TURNS) as i:
                steps[0] = 0
                for g in both:
                    ready(pool, i, g, "mv0")
                    rstd(i, g, "rstd0", twice=True)
                for g in both:
                    drained(pool, i, g, "r")
                    drained(pool, i, g, "k")
                    drained(pool, i, g, "decay")
                    tt(rk[g][:], r_sig[g][:], kF[g][:], ALU.mult).then_inc(done["rk"][g], 1)
                for l in range(LEVELS):
                    for g in both:
                        grow_k(i, g, l)
                for g in both:
                    ready(pool, i, g, "sig0")
                    drained(pool, i, g, f"y{E - 1}")
                    tt(gate0[g][:], moe[g][:], sig0[g][:], ALU.mult).then_inc(done["gate0"][g], 1)
                for g in both:
                    ready(pool, i, g, "mv1")
                    rstd(i, g, "rstd1")
                for g in both:
                    ready(pool, i, g, "sig1")
                    step(i, tt(sig1[g][:], sig1[g][:], f2[g][:], ALU.mult))
                for g in both:
                    ready(pool, i, g, "mv2")
                    rstd(i, g, "rstd2")
                for g in both:
                    ready(pool, i, g, "gate1")
                    step(i, tt(s2[g][:], s2[g][:], sig1[g][:], ALU.mult))
                    pool.wait_ge(stored[g], 16 * i + 16)
                    tt(o_out[g][:], s2[g][:], x1[g][:], ALU.add).then_inc(done["out"][g], 1)
            assert steps[0] == POOL_STEPS, steps[0]


def layout(inputs):
    f = np.float32
    a = {n: np.asarray(v) for n, v in inputs.items()}
    t = np.arange(P)
    masks = []
    for l in range(LEVELS):
        q = t[(t >> l) & 1 == 1]
        same = (t[:, None] >> (l + 1)) == (q[None, :] >> (l + 1))
        masks.append((same & ((t[:, None] >> l) & 1 == 0)).astype(f))
    return {
        "WxT": a["L0_attn_Wx"].T, "Ww": a["L0_attn_Ww"], "WvT0": a["L0_attn_Wv"].T, "Wo": a["L0_attn_Wo"],
        "Wk0": a["L0_attn_Wk"], "Wr0": a["L0_attn_Wr"],
        "routerT": a["L0_ffn_router_w"].T, "w1": a["L0_ffn_w1"],
        "w2": a["L0_ffn_w2"].reshape(E, W, P).transpose(1, 0, 2),
        "WqT": a["L1_attn_Wq"].T,
        "WkvT": np.concatenate([a["L1_attn_Wk"].T, a["L1_attn_Wv"].T], axis=1),
        "fWrT": a["L1_ffn_W_r"].T, "fWkT": a["L1_ffn_W_k"].T, "fWvT": a["L1_ffn_W_v"].T,
        "ln_g": a["L0_attn_ln_g"][:, None], "ln_b": a["L0_attn_ln_b"][:, None],
        "bw": a["L0_attn_bw"][:, None], "bq": a["L1_attn_bq"][:, None],
        "mu_r": a["L1_ffn_mu_r"][:, None], "mu_k": a["L1_ffn_mu_k"][:, None],
        "bkv": np.concatenate([a["L1_attn_bk"], a["L1_attn_bv"]])[None, :],
        "gamma": a["L1_attn_gamma"][None, :], "beta": a["L1_attn_beta"][None, :],
        "ident": np.eye(P, dtype=f), "level_mask": np.concatenate(masks, axis=1),
        "head_cols": (t[:, None] // HS == np.arange(NH)[None, :]).astype(f),
        "block_mask": (t[:, None] // AD == t[None, :] // AD).astype(f),
        "head_mask": (t[:, None] // AD == np.arange(AH)[None, :]).astype(f),
    }


def kernel(**inputs):
    import concourse.bacc as _bacc
    from concourse.bass_utils import run_bass_kernel_spmd as _run

    nc = _bacc.Bacc("TRN2", target_bir_lowering=False, num_devices=1)
    arrays = {"x": np.ascontiguousarray(inputs["L0_attn_x"])}
    for name, a in layout(inputs).items():
        arrays["in_" + name] = np.ascontiguousarray(a)
    dram = {n: nc.dram_tensor(n, a.shape, F32, kind="ExternalInput").ap() for n, a in arrays.items()}
    out = nc.dram_tensor("out", (B, T, P), F32, kind="ExternalOutput").ap()
    build(nc, dram["x"], {n[3:]: v for n, v in dram.items() if n != "x"}, out)
    r = _run(nc, [arrays], core_ids=[0])
    return r.results[0]["out"]
```

```python
from contextlib import ExitStack

import numpy as np

import concourse.bass as bass
from concourse import mybir

ALU = mybir.AluOpType
ACT = mybir.ActivationFunctionType
F32 = mybir.dt.float32
U32 = mybir.dt.uint32

P = 128
B, T = 32, 256
TILES = 4
G = TILES * P
SEQ = G // T
CH = T // P
LANES = 2
TURNS = B * T // (LANES * G)
NH, HS = 2, 64
LEVELS = 7
E, W = 8, 128
AH, AD = 16, 8
EPS = 1e-5
EPS_DENOM = 1e-6

FILLS = {
    "c0": ["xnT", "decay", "r", "vw_hi", "level0", "level2", "level4", "level6", "y"],
    "c1": ["znT", "k", "route_diag", "vw_lo", "level1", "level3", "level5", "level7"],
    "h": [f"h{e}" for e in range(E)] + ["q", "kv_hi", "ffn_r", "ffn_v", "ctx_hi"],
    "y": [f"y{e}" for e in range(E)] + ["xn1T", "kv_lo", "ffn_k", "kvm", "ctx_lo"],
}
WHERE = {name: (bank, n + 1) for bank, names in FILLS.items() for n, name in enumerate(names)}

COLUMNS = ["ln_g", "ln_b", "bw", "bq", "mu_r", "mu_k"]
ROWS = ["bkv", "gamma", "beta"]


STATS_AT = (3, 4)
BIAS_AT = (4, 5)
NORM_AT = (5, 6)
OUT_AT = (1, 2)
ACT_WEIGHS = (0, 1, 2, 3)
EARLY = ["WxT", "Ww", "WvT0", "Wo", "bw", "ident", "ln_g", "ln_b", "Wk0", "Wr0", "routerT", "head_cols",
         "level_mask"]


def passing(eng, signal, per):
    n = [0]

    def step(i, ins):
        n[0] = n[0] % per + 1
        ins.then_inc(signal, 1)
        eng.wait_ge(signal, i * per + n[0])
    return step, n


def build(nc, x, w, out):
    x_tiles = x.rearrange("b (c p) d -> p (b c) d", p=P)
    out_tiles = out.rearrange("b (c p) d -> p (b c) d", p=P)

    with ExitStack() as ctx:
        def sb(name, shape, dt=F32):
            return ctx.enter_context(nc.sbuf_tensor(name, shape, dt))

        def lanes(name, shape, dt=F32):
            return [sb(f"{name}{g}", shape, dt) for g in range(LANES)]

        def sem(name):
            return ctx.enter_context(nc.semaphore(name))

        def sems(name):
            return [sem(f"{name}{g}") for g in range(LANES)]

        WT = {n: sb("w_" + n, list(w[n].shape)) for n in w if n not in COLUMNS + ROWS}
        COL = {n: sb("c_" + n, [P, 1]) for n in COLUMNS}
        ROW = {n: sb("r_" + n, [P, w[n].shape[1]]) for n in ROWS}
        neg_bw = sb("neg_bw", [P, 1])
        warm = sb("warm", [P, 1])
        w_decay = sb("w_decay", [P, P])
        w_vo = sb("w_vo", [P, NH * P])
        minus_half = sb("minus_half", [P, 2, TILES])

        x_in = lanes("x_in", [P, TILES, P])
        x_res = lanes("x_res", [P, TILES, P])
        stats = lanes("stats", [P, TILES, 6])
        mv = lanes("mv", [P, TILES, 2])
        ve = lanes("ve", [P, TILES])
        rs = lanes("rs", [P, TILES])
        stats_x = lanes("stats_x", [P, TILES, 6])
        mv_x = lanes("mv_x", [P, TILES, 2])
        ve_x = lanes("ve_x", [P, 2, TILES])
        inv_x = lanes("inv_x", [P, TILES])
        rs_x = lanes("rs_x", [P, 2, TILES])
        bias_x = lanes("bias_x", [P, TILES])
        weighted = [lanes(f"weighted{n}_", [P, TILES, P]) for n in range(2)]
        xn = lanes("xn", [P, TILES, P])
        zn = lanes("zn", [P, TILES, P])
        xnT = lanes("xnT", [P, G])
        znT = lanes("znT", [P, G])
        decay = lanes("decay", [P, G])
        r_sig = lanes("r_sig", [P, G])
        kF = lanes("kF", [P, G])
        rF = lanes("rF", [P, NH, G])
        rk = lanes("rk", [P, G])
        tot = [lanes(f"tot{l}_", [P, G >> l]) for l in range(1, LEVELS)]
        a_diag = lanes("a_diag", [P, TILES, NH, P])
        a_off = lanes("a_off", [P, SEQ, NH, P])
        vw = lanes("vw", [P, TILES, NH * P])
        probs = lanes("probs", [P, TILES, 16])
        top = lanes("top", [P, TILES, E])
        pick = lanes("pick", [P, TILES, E])
        rest = lanes("rest", [P, TILES, 16])
        den = lanes("den", [P, TILES])
        cw = lanes("cw", [P, TILES, E])
        u = lanes("u", [P, G])
        act_sq = lanes("act_sq", [P, G])
        moe = lanes("moe", [P, TILES, P])
        sig0 = lanes("sig0", [P, TILES, P])
        gate0 = lanes("gate0", [P, TILES, P])
        x1 = lanes("x1", [P, TILES, P])
        xn1 = lanes("xn1", [P, TILES, P])
        xn1T = lanes("xn1T", [P, SEQ, T + 1])
        diff = lanes("diff", [P, SEQ, T])
        xr = lanes("xr", [P, SEQ, T])
        xk = lanes("xk", [P, SEQ, T])
        qT = lanes("qT", [P, G])
        k_pre = lanes("k_pre", [P, TILES, P])
        k_tok = lanes("k_tok", [P, TILES, P])
        v_tok = lanes("v_tok", [P, TILES, P + 1])
        kvm = lanes("kvm", [P, SEQ, P + AH])
        rden = lanes("rden", [P, TILES, AH])
        dmax = lanes("dmax", [P, TILES, AH])
        att = lanes("att", [P, TILES, P])
        ysum = lanes("ysum", [P, TILES, P])
        centred = att
        s2 = lanes("s2", [P, TILES, P])
        gate1 = lanes("gate1", [P, TILES, P])
        r2 = lanes("r2", [P, TILES, P])
        ku = lanes("ku", [P, G])
        ksq = lanes("ksq", [P, G])
        f2 = lanes("f2", [P, TILES, P])
        sig1 = lanes("sig1", [P, TILES, P])
        o_out = lanes("o_out", [P, TILES, P])

        bank = {b: [ctx.enter_context(nc.psum_tensor(f"bank_{b}{g}", [P, 512], F32))
                    for g in range(LANES)] for b in FILLS}
        filled = {b: sems(f"filled_{b}") for b in FILLS}
        free = {b: sems(f"free_{b}") for b in FILLS}

        early_loaded = sem("early_loaded")
        loaded = sem("loaded")
        prep_mm = sem("prep_mm")
        prep_done = sem("prep_done")
        dve_set = sem("dve_set")
        pool_set = sem("pool_set")
        x_loaded = sems("x_loaded")
        res_loaded = sems("res_loaded")
        stored = sems("stored")
        dve_step, dve_front_step = sem("dve_step"), sem("dve_front_step")
        dve_passed = sem("dve_passed")
        names = ["act_sq", "bias0", "cw", "gate0", "gate1", "kF_level", "k_pre", "k_tok", "ksq", "moe", "mv0", "mv1", "mv2", "out", "probs", "rF0", "rF_level", "rk", "rstd0", "rstd1", "rstd2", "s2", "sig0", "sig1", "tot_level", "x1", "xk", "xn", "xn1", "xr", "zn"]
        done = {n: sems(n + "_done") for n in names}

        block = ctx.enter_context(nc.Block())

        def full(eng, i, g, name):
            b, k = WHERE[name]
            eng.wait_ge(filled[b][g], i * len(FILLS[b]) + k)

        def writable(eng, i, g, name):
            b, k = WHERE[name]
            eng.wait_ge(free[b][g], i * len(FILLS[b]) + k)

        def drained(eng, i, g, name):
            b, k = WHERE[name]
            eng.wait_ge(free[b][g], i * len(FILLS[b]) + k + 1)

        def stand_alone(eng):
            eng.sem_inc(dve_passed, 1)

        def fills(ins, g, name):
            ins.then_inc(filled[WHERE[name][0]][g], 1)

        def drains(ins, g, name):
            ins.then_inc(free[WHERE[name][0]][g], 1)

        def at(name, g):
            return bank[WHERE[name][0]][g]

        def ready(eng, i, g, name, k=1, per=1):
            eng.wait_ge(done[name][g], i * per + k)

        n_early, n_late = len(EARLY), len(w) - len(EARLY)

        @block.sync
        def _(sp):
            def load(i):
                for g in range(LANES):
                    tiles = x_tiles[:, bass.ds(i * (LANES * TILES) + g * TILES, TILES), :]
                    sp.dma_start(x_in[g][:], tiles).then_inc(x_loaded[g], 16)

            def load_res(i):
                for g in range(LANES):
                    tiles = x_tiles[:, bass.ds(i * (LANES * TILES) + g * TILES, TILES), :]
                    sp.dma_start(x_res[g][:], tiles).then_inc(res_loaded[g], 16)

            def store(i):
                for g in range(LANES):
                    ready(sp, i, g, "out")
                    sp.dma_start(out_tiles[:, bass.ds(i * (LANES * TILES) + g * TILES, TILES), :],
                                 o_out[g][:]).then_inc(stored[g], 16)

            def x_in_used(i):
                for g in range(LANES):
                    ready(sp, i, g, "xn")

            def x_res_used(i):
                for g in range(LANES):
                    ready(sp, i, g, "x1")

            load(0)
            for n in EARLY + [n for n in w if n not in EARLY]:
                dst = COL[n][:] if n in COLUMNS else ROW[n][:] if n in ROWS else WT[n][:]
                src = w[n].to_broadcast([P, w[n].shape[1]]) if n in ROWS else w[n]
                sp.dma_start(dst, src).then_inc(early_loaded if n in EARLY else loaded, 16)
            load_res(0)
            x_in_used(0)
            load(1)
            with sp.Fori(1, TURNS - 1) as i:
                x_in_used(i)
                load(i + 1)
                x_res_used(i - 1)
                load_res(i)
                store(i - 1)
            x_res_used(TURNS - 2)
            load_res(TURNS - 1)
            store(TURNS - 2)
            store(TURNS - 1)
            for g in range(LANES):
                sp.wait_ge(stored[g], 16 * TURNS + 16)

        @block.tensor
        def _(pe):
            mm = nc.tensor.matmul
            pe.wait_ge(early_loaded, 16 * n_early)
            mm(bank["c0"][0][:, 0:P], WT["WxT"][:], WT["Ww"][:], start=True, stop=True)
            for h in range(NH):
                rows = slice(h * HS, (h + 1) * HS)
                last = mm(bank["h" if h else "c1"][0][:, 0:P], WT["WvT0"][rows, :], WT["Wo"][rows, :],
                          start=True, stop=True)
            last.then_inc(prep_mm, 1)
            pe.wait_ge(prep_done, 4)

            def transposes(i, g, name, src):
                writable(pe, i, g, name)
                for j in range(TILES):
                    last = nc.tensor.transpose(at(name, g)[:, j * P:(j + 1) * P], src[:, j, :], WT["ident"][:])
                fills(last, g, name)

            def product(i, g, name, weight, moving):
                writable(pe, i, g, name)
                fills(mm(at(name, g)[:], weight, moving, start=True, stop=True), g, name)

            def token_product(i, g, name, tokT, weight, tiles, step):
                writable(pe, i, g, name)
                n = weight.shape[1]
                for m, j in enumerate(tiles):
                    last = mm(at(name, g)[:, m * step:m * step + n], tokT[:, j * P:(j + 1) * P], weight,
                              start=True, stop=True)
                fills(last, g, name)

            def route_diag(i, g):
                writable(pe, i, g, "route_diag")
                ps = at("route_diag", g)
                for j in range(TILES):
                    mm(ps[:, j * E:(j + 1) * E], xnT[g][:, j * P:(j + 1) * P], WT["routerT"][:],
                       start=True, stop=True)
                ready(pe, i, g, "rk")
                for j in range(TILES):
                    last = mm(ps[:, 64 + j * NH:64 + (j + 1) * NH], rk[g][:, j * P:(j + 1) * P],
                              WT["head_cols"][:], start=True, stop=True)
                fills(last, g, "route_diag")

            def level(i, g, l):
                name = f"level{l}"
                if l == 0:
                    drained(pe, i, g, "k")
                    ready(pe, i, g, "rF0")
                else:
                    ready(pe, i, g, "kF_level", l, LEVELS)
                    ready(pe, i, g, "rF_level", l, LEVELS)
                writable(pe, i, g, name)
                ps = at(name, g)
                if l < LEVELS:
                    half = 1 << l
                    for j in range(TILES):
                        q = rF[g][:, :, j * P:(j + 1) * P].rearrange("p h (n two k) -> p h n two k",
                                                                     two=2, k=half)[:, :, :, 1, :]
                        last = mm(ps[:, j * P:(j + 1) * P], kF[g][:, j * P:(j + 1) * P], q,
                                  start=True, stop=True)
                else:
                    for s in range(SEQ):
                        j = s * CH
                        last = mm(ps[:, s * NH * P:(s + 1) * NH * P], kF[g][:, j * P:(j + 1) * P],
                                  rF[g][:, :, (j + 1) * P:(j + 2) * P], start=True, stop=True)
                fills(last, g, name)

            def expert_in(i, g, e):
                product(i, g, f"h{e}", WT["w1"][:, e * W:(e + 1) * W], xnT[g][:])

            def expert_out(i, g, e):
                name = f"y{e}"
                writable(pe, i, g, name)
                ready(pe, i, g, "act_sq", e + 1, E)
                for j in range(TILES):
                    last = mm(at(name, g)[:, j * P:(j + 1) * P], act_sq[g][:, j * P:(j + 1) * P],
                              WT["w2"][:, e, :], start=True, stop=True)
                fills(last, g, name)

            def mix(i, g):
                writable(pe, i, g, "y")
                drained(pe, i, g, "level7")
                for j in range(TILES):
                    o = at("y", g)[:, j * P:(j + 1) * P]
                    parts = [(a_diag[g][:, j, h, :], vw[g][:, j, h * P:(h + 1) * P]) for h in range(NH)]
                    if j % CH:
                        parts += [(a_off[g][:, j // CH, h, :], vw[g][:, j - 1, h * P:(h + 1) * P])
                                  for h in range(NH)]
                    for n, (s, v) in enumerate(parts):
                        last = mm(o, s, v, start=(n == 0), stop=(n == len(parts) - 1))
                fills(last, g, "y")

            def kv_sums(i, g):
                writable(pe, i, g, "kvm")
                ready(pe, i, g, "k_tok", 2, 2)
                drained(pe, i, g, "kv_hi")
                for s in range(SEQ):
                    for c in range(CH):
                        j = s * CH + c
                        last = mm(at("kvm", g)[:, s * 256:s * 256 + P + 1], k_tok[g][:, j, :],
                                  v_tok[g][:, j, :], start=(c == 0), stop=(c == CH - 1))
                fills(last, g, "kvm")

            def context(i, g, name, tiles):
                writable(pe, i, g, name)
                drained(pe, i, g, "q")
                drained(pe, i, g, "kvm")
                for m, j in enumerate(tiles):
                    last = mm(at(name, g)[:, m * 256:m * 256 + P + AH], qT[g][:, j * P:(j + 1) * P],
                              kvm[g][:, j // CH, :], start=True, stop=True)
                fills(last, g, name)

            both = range(LANES)

            def front_first(i):
                for g in both:
                    ready(pe, i, g, "xn")
                    transposes(i, g, "xnT", xn[g])
                    ready(pe, i, g, "zn")
                    transposes(i, g, "znT", zn[g])
                for g in both:
                    drained(pe, i, g, "znT")
                    product(i, g, "decay", w_decay[:], znT[g][:])
                    product(i, g, "k", WT["Wk0"][:], znT[g][:])
                for g in both:
                    product(i, g, "r", WT["Wr0"][:], znT[g][:])

            def front_values(i):
                for g in both:
                    token_product(i, g, "vw_lo", znT[g], w_vo[:], range(0, 2), NH * P)
                    token_product(i, g, "vw_hi", znT[g], w_vo[:], range(2, 4), NH * P)

            def front_route(i, g):
                drained(pe, i, g, "xnT")
                route_diag(i, g)

            def front_level(i):
                for g in both:
                    level(i, g, 0)

            def main(i):
                for g in both:
                    drained(pe, i, g, "xnT")
                    expert_in(i, g, 0)
                for n in range(E):
                    if n:
                        for g in both:
                            level(i, g, n)
                    for g in both:
                        expert_out(i, g, n)
                    if n + 1 < E:
                        for g in both:
                            expert_in(i, g, n + 1)
                for g in both:
                    mix(i, g)

            def tail_start(i):
                for g in both:
                    ready(pe, i, g, "xn1")
                    transposes(i, g, "xn1T", xn1[g])
                for g in both:
                    drained(pe, i, g, "xn1T")
                    writable(pe, i, g, "q")
                    fills(mm(at("q", g)[:], WT["WqT"][:], xn1T[g][:, :, 1:], start=True, stop=True), g, "q")
                    for name, tiles in (("kv_lo", (0, 1)), ("kv_hi", (2, 3))):
                        writable(pe, i, g, name)
                        for m, j in enumerate(tiles):
                            c = 1 + (j % CH) * P
                            last = mm(at(name, g)[:, m * 256:(m + 1) * 256], xn1T[g][:, j // CH, c:c + P],
                                      WT["WkvT"][:], start=True, stop=True)
                        fills(last, g, name)

            def tail_ffn(i, g):
                ready(pe, i, g, "xk")
                product(i, g, "ffn_k", WT["fWkT"][:], xk[g][:].rearrange("p s t -> p (s t)"))
                ready(pe, i, g, "xr")
                token_product(i, g, "ffn_r", xr[g][:].rearrange("p s t -> p (s t)"), WT["fWrT"][:],
                              range(TILES), P)

            def tail_sums(i):
                for g in both:
                    kv_sums(i, g)

            def tail_end(i):
                for g in both:
                    ready(pe, i, g, "ksq")
                    token_product(i, g, "ffn_v", ksq[g], WT["fWvT"][:], range(TILES), P)
                for g in both:
                    context(i, g, "ctx_lo", (0, 1))
                    context(i, g, "ctx_hi", (2, 3))

            front_first(0)
            for g in both:
                front_route(0, g)
            front_values(0)
            pe.wait_ge(dve_set, 2)
            pe.wait_ge(pool_set, 1)
            front_level(0)
            pe.wait_ge(loaded, 16 * n_late)

            def turn(i):
                main(i)
                front_first(i + 1)
                tail_start(i)
                for g in both:
                    front_route(i + 1, g)
                    tail_ffn(i, g)
                front_values(i + 1)
                tail_sums(i)
                front_level(i + 1)
                tail_end(i)

            turn(0)
            with pe.Fori(1, TURNS - 1) as i:
                turn(i)
            main(TURNS - 1)
            tail_start(TURNS - 1)
            for g in both:
                tail_ffn(TURNS - 1, g)
            tail_sums(TURNS - 1)
            tail_end(TURNS - 1)

        @block.scalar
        def _(act):
            af = nc.scalar.activation
            act.wait_ge(early_loaded, 16 * n_early)
            af(warm[:], COL["bw"][:], ACT.Sigmoid)
            nc.scalar.mul(neg_bw[:], COL["bw"][:], -1.0).then_inc(prep_done, 1)
            act.wait_ge(prep_mm, 1)
            nc.scalar.copy(w_decay[:], bank["c0"][0][:, 0:P]).then_inc(prep_done, 1)
            nc.scalar.copy(w_vo[:, 0:P], bank["c1"][0][:, 0:P]).then_inc(prep_done, 1)
            nc.scalar.copy(w_vo[:, P:2 * P], bank["h"][0][:, 0:P]).then_inc(prep_done, 1)
            act.wait_ge(prep_done, 4)

            def drain(i, g, name, o, func, **kw):
                full(act, i, g, name)
                drains(af(o, at(name, g)[:], func, **kw), g, name)

            def expert_act(i, g, e):
                drain(i, g, f"h{e}", u[g][:], ACT.Relu)
                drained(act, i, g, f"h{e}")
                if e:
                    b, k = WHERE[f"y{e - 1}"]
                    act.wait_ge(filled[b][g], i * len(FILLS[b]) + k)
                af(act_sq[g][:], u[g][:], ACT.Square).then_inc(done["act_sq"][g], 1)

            def weigh(i, g, e):
                full(act, i, g, f"y{e}")
                if e == ACT_WEIGHS[0]:
                    ready(act, i, g, "cw")
                if e > 2:
                    ready(act, i, g, "moe", e - 2, E - 1)
                o = weighted[e % 2][g] if e else moe[g]
                for j in range(TILES):
                    last = af(o[:, j, :], at(f"y{e}", g)[:, j * P:(j + 1) * P], ACT.Copy,
                              scale=cw[g][:, j, e:e + 1])
                drains(last, g, f"y{e}")

            both = range(LANES)

            def front_norm(i, g):
                ready(act, i, g, "bias0")
                for j in range(TILES):
                    last = af(xn[g][:, j, :], x_in[g][:, j, :], ACT.Identity, scale=rs_x[g][:, 0, j:j + 1],
                              bias=bias_x[g][:, j:j + 1])
                last.then_inc(done["xn"][g], 1)
                ready(act, i, g, "xn")
                for j in range(TILES):
                    last = af(zn[g][:, j, :], xn[g][:, j, :], ACT.Copy, scale=rs_x[g][:, 1, j:j + 1])
                last.then_inc(done["zn"][g], 1)

            def front_first(i):
                for g in both:
                    drain(i, g, "xnT", xnT[g][:], ACT.Copy)
                    drain(i, g, "znT", znT[g][:], ACT.Identity, bias=COL["ln_b"][:], scale=COL["ln_g"][:])
                for g in both:
                    drain(i, g, "decay", decay[g][:], ACT.Sigmoid, bias=neg_bw[:], scale=-1.0)
                    drain(i, g, "k", kF[g][:], ACT.Copy)
                for g in both:
                    drain(i, g, "r", r_sig[g][:], ACT.Sigmoid)

            def front_values(i):
                for g in both:
                    drain(i, g, "vw_lo", vw[g][:, 0:2, :].rearrange("p j n -> p (j n)"), ACT.Copy)
                    drain(i, g, "vw_hi", vw[g][:, 2:4, :].rearrange("p j n -> p (j n)"), ACT.Copy)

            def front_route(i, g):
                full(act, i, g, "route_diag")
                af(probs[g][:, :, 0:E], at("route_diag", g)[:, 0:TILES * E].rearrange(
                    "p (j e) -> p j e", e=E), ACT.Sigmoid).then_inc(done["probs"][g], 1)

            def main(i, next_front):
                for e in range(E):
                    for g in both:
                        expert_act(i, g, e)
                    for g in both:
                        if e in ACT_WEIGHS:
                            weigh(i, g, e)
                    for g in both:
                        if e == NORM_AT[g] and next_front:
                            front_norm(i + 1, g)
                for g in both:
                    drain(i, g, "level7", a_off[g][:].rearrange("p s h t -> p (s h t)"), ACT.Copy)
                for g in both:
                    ready(act, i, g, "moe", E - 1, E - 1)
                    af(sig0[g][:], moe[g][:], ACT.Sigmoid).then_inc(done["sig0"][g], 1)

            def tail_start(i):
                for g in both:
                    full(act, i, g, "xn1T")
                    for s in range(SEQ):
                        ins = af(xn1T[g][:, s, 1:], at("xn1T", g)[:, s * T:(s + 1) * T], ACT.Copy)
                    drains(ins, g, "xn1T")
                for g in both:
                    drain(i, g, "q", qT[g][:], ACT.Relu, bias=COL["bq"][:])
                for g in both:
                    for m in range(2):
                        ready(act, i, g, "k_pre", m + 1, 2)
                        af(k_tok[g][:, 2 * m:2 * m + 2, :], k_pre[g][:, 2 * m:2 * m + 2, :], ACT.Relu
                           ).then_inc(done["k_tok"][g], 1)

            def tail_ffn(i, g):
                drain(i, g, "ffn_k", ku[g][:], ACT.Relu)
                drained(act, i, g, "ffn_k")
                af(ksq[g][:], ku[g][:], ACT.Square).then_inc(done["ksq"][g], 1)
                drain(i, g, "ffn_r", r2[g][:].rearrange("p j n -> p (j n)"), ACT.Sigmoid)

            def tail_end(i):
                for g in both:
                    drained(act, i, g, "ffn_v")
                    af(sig1[g][:], f2[g][:], ACT.Sigmoid).then_inc(done["sig1"][g], 1)

            for g in both:
                front_norm(0, g)
            front_first(0)
            act.wait_ge(pool_set, 1)
            for g in both:
                front_route(0, g)
            front_values(0)
            act.wait_ge(loaded, 16 * n_late)

            def turn(i):
                main(i, True)
                front_first(i + 1)
                tail_start(i)
                for g in both:
                    front_route(i + 1, g)
                    tail_ffn(i, g)
                front_values(i + 1)
                tail_end(i)

            turn(0)
            with act.Fori(1, TURNS - 1) as i:
                turn(i)
            main(TURNS - 1, False)
            tail_start(TURNS - 1)
            for g in both:
                tail_ffn(TURNS - 1, g)
            tail_end(TURNS - 1)

        DVE_STEPS, DVE_FRONT_STEPS = LANES * 12, LANES * 9

        @block.vector
        def _(dve):
            tt, ts, stt = nc.vector.tensor_tensor, nc.vector.tensor_scalar, nc.vector.scalar_tensor_tensor
            nc.vector.memset(minus_half[:], -0.5)
            for g in range(LANES):
                last = nc.vector.memset(rF[g][:], 0.0)
            last.then_inc(dve_set, 1)
            step, steps = passing(dve, dve_step, DVE_STEPS)
            front_step, front_steps = passing(dve, dve_front_step, DVE_FRONT_STEPS)

            def moments(i, g, src, st, out, passed_on):
                for j in range(TILES):
                    last = nc.vector.bn_stats(st[g][:, j, :], src[:, j, :])
                passed_on(i, last)
                stand_alone(dve)
                for j in range(TILES):
                    last = nc.vector.bn_aggr(out[g][:, j, :], st[g][:, j, :])
                passed_on(i, last)

            def tail_moments(i, g, src, name):
                moments(i, g, src, stats, mv, step)
                ts(ve[g][:], mv[g][:, :, 1], EPS, None, ALU.add).then_inc(done[name][g], 1)

            def normalise(i, g, o, src, mean, scale, name):
                for j in range(TILES):
                    last = ts(o[:, j, :], src[:, j, :], mean[:, j:j + 1], scale[:, j:j + 1],
                              ALU.subtract, ALU.mult)
                last.then_inc(done[name][g], 1)

            def level_scores(i, g, l):
                half = 1 << l
                full(dve, i, g, f"level{l}")
                drained(dve, i, g, f"level{l - 1}" if l else "route_diag")
                o = a_diag[g][:].rearrange("p j h (n two k) -> p (j h) n two k", two=2, k=half)[:, :, :, 1, :]
                ps = at(f"level{l}", g)[:].rearrange("p (m n k) -> p m n k", m=TILES * NH, k=half)
                m = WT["level_mask"][:, l * HS:(l + 1) * HS].bitcast(U32).rearrange(
                    "p (n k) -> p n k", k=half).unsqueeze(1).to_broadcast([P, TILES * NH, HS // half, half])
                stand_alone(dve)
                ins = nc.vector.copy_predicated(o, m, ps)
                drains(ins, g, f"level{l}")

            def grow_r(i, g, l):
                half = 1 << l
                full(dve, i, g, f"level{l}")
                if l:
                    ready(dve, i, g, "tot_level", l, LEVELS - 1)
                    dve.wait_ge(done["rF_level"][g], i * LEVELS + l)
                t = decay[g] if l == 0 else tot[l - 1][g]
                right = rF[g][:].rearrange("p h (n two k) -> p h n two k", two=2, k=half)[:, :, :, 1, :]
                left_tot = t[:].rearrange("p (n two) -> p n two", two=2)[:, :, 0:1]
                left_tot = left_tot.unsqueeze(1).to_broadcast([P, NH, G // (2 * half), half])
                tt(right, right, left_tot, ALU.mult).then_inc(done["rF_level"][g], 1)

            def weigh(i, g, e):
                full(dve, i, g, f"y{e}")
                if e > 2:
                    ready(dve, i, g, "moe", e - 2, E - 1)
                o = weighted[e % 2][g] if e else moe[g]
                drains(tt(o[:], at(f"y{e}", g)[:].rearrange("p (j n) -> p j n", j=TILES),
                          cw[g][:, :, e:e + 1].to_broadcast([P, TILES, P]), ALU.mult), g, f"y{e}")

            def route(i, g):
                ready(dve, i, g, "probs")
                stand_alone(dve)
                for j in range(TILES):
                    last = nc.vector.max(top[g][:, j, :], probs[g][:, j, 0:E])
                front_step(i, last)
                nc.vector.tensor_copy(pick[g][:, :, 0:2], top[g][:, :, 0:2])
                front_step(i, tt(den[g][:], top[g][:, :, 0], top[g][:, :, 1], ALU.add))
                ts(den[g][:], den[g][:], 1e-20, None, ALU.add)
                for j in range(TILES):
                    last = nc.vector.match_replace(rest[g][:, j, :], pick[g][:, j, :], probs[g][:, j, :], 0.0)
                front_step(i, last)
                nc.vector.reciprocal(den[g][:], den[g][:])
                front_step(i, tt(cw[g][:], probs[g][:, :, 0:E], rest[g][:, :, 0:E], ALU.subtract))
                tt(cw[g][:], cw[g][:], den[g][:].unsqueeze(2).to_broadcast([P, TILES, E]), ALU.mult
                   ).then_inc(done["cw"][g], 1)
                ready(dve, i, g, "cw")

            both = range(LANES)

            def front_stats(i, g):
                dve.wait_ge(x_loaded[g], 16 * i + 16)
                moments(i, g, x_in[g], stats_x, mv_x, front_step)
                var = mv_x[g][:, :, 1]
                front_step(i, ts(ve_x[g][:, 0, :], var, EPS, None, ALU.add))
                front_step(i, nc.vector.reciprocal(inv_x[g][:], ve_x[g][:, 0, :]))
                front_step(i, tt(inv_x[g][:], inv_x[g][:], var, ALU.mult))
                ts(ve_x[g][:, 1, :], inv_x[g][:], EPS, None, ALU.add).then_inc(done["mv0"][g], 1)

            def front_bias(i, g):
                ready(dve, i, g, "rstd0")
                stt(bias_x[g][:], mv_x[g][:, :, 0], -1.0, rs_x[g][:, 0, :], ALU.mult, ALU.mult
                    ).then_inc(done["bias0"][g], 1)

            def front_r(i):
                for g in both:
                    drained(dve, i, g, "r")
                    drained(dve, i, g, "decay")
                    for h in range(NH):
                        rows = slice(h * HS, (h + 1) * HS)
                        last = tt(rF[g][rows, h, :], r_sig[g][rows, :], decay[g][rows, :], ALU.mult)
                    last.then_inc(done["rF0"][g], 1)

            def front_diag(i):
                for g in both:
                    full(dve, i, g, "route_diag")
                    ready(dve, i, g, "probs")
                    d = at("route_diag", g)[:, 64:64 + TILES * NH].unsqueeze(2).to_broadcast([P, TILES * NH, P])
                    m = WT["ident"][:].bitcast(U32).unsqueeze(1).to_broadcast([P, TILES * NH, P])
                    stand_alone(dve)
                    ins = nc.vector.copy_predicated(a_diag[g][:].rearrange("p j h t -> p (j h) t"), m, d)
                    drains(ins, g, "route_diag")

            def front_route(i):
                for g in both:
                    route(i, g)

            def start(i):
                for g in both:
                    ready(dve, i, g, "rF0")
                    grow_r(i, g, 0)
                    level_scores(i, g, 0)

            def main(i, next_front, last_out=True):
                for n in range(E):
                    for g in both:
                        if 0 < n < LEVELS:
                            grow_r(i, g, n)
                            level_scores(i, g, n)
                    for g in both:
                        if n not in ACT_WEIGHS:
                            weigh(i, g, n)
                    for g in both:
                        if last_out and n == OUT_AT[g]:
                            tail_out(i - 1, g)
                        if next_front and n == STATS_AT[g]:
                            front_stats(i + 1, g)
                        if next_front and n == BIAS_AT[g]:
                            front_bias(i + 1, g)

            def tail_x1(i):
                for g in both:
                    ready(dve, i, g, "gate0")
                    full(dve, i, g, "y")
                    drains(tt(x1[g][:].rearrange("p j n -> p (j n)"), at("y", g)[:],
                              gate0[g][:].rearrange("p j n -> p (j n)"), ALU.mult), g, "y")
                for g in both:
                    drained(dve, i, g, "y")
                    dve.wait_ge(res_loaded[g], 16 * i + 16)
                    tt(x1[g][:], x1[g][:], x_res[g][:], ALU.add).then_inc(done["x1"][g], 1)
                    ready(dve, i, g, "x1")
                    tail_moments(i, g, x1[g], "mv1")

            def tail_xn1(i):
                for g in both:
                    ready(dve, i, g, "rstd1")
                    normalise(i, g, xn1[g], x1[g], mv[g][:, :, 0], rs[g][:], "xn1")

            def tail_shift(i, g):
                drained(dve, i, g, "xn1T")
                prev = xn1T[g][:, :, 0:T]
                step(i, tt(diff[g][:], xn1T[g][:, :, 1:], prev, ALU.subtract))
                stt(xk[g][:], diff[g][:], COL["mu_k"][:], prev, ALU.mult, ALU.add
                    ).then_inc(done["xk"][g], 1)
                stt(xr[g][:], diff[g][:], COL["mu_r"][:], prev, ALU.mult, ALU.add
                    ).then_inc(done["xr"][g], 1)

            def tail_kv(i, g):
                for m, name in enumerate(("kv_lo", "kv_hi")):
                    full(dve, i, g, name)
                    ps = at(name, g)[:].rearrange("p (j n) -> p j n", n=2 * P)
                    js = slice(2 * m, 2 * m + 2)
                    tt(k_pre[g][:, js, :], ps[:, :, 0:P],
                       ROW["bkv"][:, 0:P].unsqueeze(1).to_broadcast([P, 2, P]), ALU.add
                       ).then_inc(done["k_pre"][g], 1)
                    drains(tt(v_tok[g][:, js, 0:P], ps[:, :, P:2 * P],
                              ROW["bkv"][:, P:2 * P].unsqueeze(1).to_broadcast([P, 2, P]), ALU.add),
                           g, name)

            def tail_kvm(i):
                for g in both:
                    full(dve, i, g, "kvm")
                    ps = at("kvm", g)[:].rearrange("p (s n) -> p s n", n=256)
                    tt(kvm[g][:, :, 0:P], ps[:, :, 0:P],
                       WT["block_mask"][:].unsqueeze(1).to_broadcast([P, SEQ, P]), ALU.mult)
                    drains(tt(kvm[g][:, :, P:], ps[:, :, P:P + 1].to_broadcast([P, SEQ, AH]),
                              WT["head_mask"][:].unsqueeze(1).to_broadcast([P, SEQ, AH]), ALU.mult), g, "kvm")

            def tail_f2(i):
                for g in both:
                    full(dve, i, g, "ffn_v")
                    drained(dve, i, g, "ffn_r")
                    drains(tt(f2[g][:].rearrange("p j n -> p (j n)"), at("ffn_v", g)[:],
                              r2[g][:].rearrange("p j n -> p (j n)"), ALU.mult), g, "ffn_v")

            def tail_ctx(i):
                for g in both:
                    for m, name in enumerate(("ctx_lo", "ctx_hi")):
                        js = slice(2 * m, 2 * m + 2)
                        full(dve, i, g, name)
                        ps = at(name, g)[:].rearrange("p (j n) -> p j n", n=256)
                        step(i, ts(dmax[g][:, js, :], ps[:, :, P:P + AH], EPS_DENOM, None, ALU.max))
                        step(i, nc.vector.reciprocal(rden[g][:, js, :], dmax[g][:, js, :]))
                        drains(tt(att[g][:, js, :].rearrange("p j (h d) -> p j h d", d=AD),
                                  ps[:, :, 0:P].rearrange("p j (h d) -> p j h d", d=AD),
                                  rden[g][:, js, :].unsqueeze(3).to_broadcast([P, 2, AH, AD]), ALU.mult),
                               g, name)

            def tail_sum(i):
                for g in both:
                    drained(dve, i, g, "ctx_lo")
                    drained(dve, i, g, "ctx_hi")
                    step(i, tt(ysum[g][:], att[g][:], xn1[g][:], ALU.add))
                    tail_moments(i, g, ysum[g], "mv2")

            def tail_out(i, g):
                ready(dve, i, g, "rstd2")
                for j in range(TILES):
                    last = stt(centred[g][:, j, :], ysum[g][:, j, :], mv[g][:, j, 0:1], ROW["gamma"][:],
                               ALU.subtract, ALU.mult)
                step(i, last)
                for j in range(TILES):
                    last = stt(s2[g][:, j, :], centred[g][:, j, :], rs[g][:, j:j + 1], ROW["beta"][:],
                               ALU.mult, ALU.add)
                step(i, last)
                ready(dve, i, g, "gate1")
                tt(s2[g][:], s2[g][:], gate1[g][:], ALU.mult).then_inc(done["s2"][g], 1)

            for g in both:
                front_stats(0, g)
            dve.wait_ge(prep_done, 4)
            for g in both:
                for b in FILLS:
                    dve.sem_inc(free[b][g], 1)
                dve.sem_inc(stored[g], 16)
            for g in both:
                front_bias(0, g)
            for g in both:
                last = nc.vector.memset(a_diag[g][:], 0.0)
            last.then_inc(dve_set, 1)
            dve.wait_ge(dve_set, 2)
            dve.wait_ge(pool_set, 1)
            dve.wait_ge(early_loaded, 16 * n_early)
            front_r(0)
            front_diag(0)
            front_route(0)
            start(0)
            dve.wait_ge(loaded, 16 * n_late)

            def turn(i, last_out=True):
                main(i, True, last_out)
                tail_x1(i)
                tail_xn1(i)
                for g in both:
                    tail_shift(i, g)
                for g in both:
                    tail_kv(i, g)
                front_r(i + 1)
                front_diag(i + 1)
                front_route(i + 1)
                tail_kvm(i)
                start(i + 1)
                tail_f2(i)
                tail_ctx(i)
                tail_sum(i)

            turn(0, last_out=False)
            with dve.Fori(1, TURNS - 1) as i:
                turn(i)
            main(TURNS - 1, False)
            tail_x1(TURNS - 1)
            tail_xn1(TURNS - 1)
            for g in both:
                tail_shift(TURNS - 1, g)
            for g in both:
                tail_kv(TURNS - 1, g)
            tail_kvm(TURNS - 1)
            tail_f2(TURNS - 1)
            tail_ctx(TURNS - 1)
            tail_sum(TURNS - 1)
            for g in both:
                tail_out(TURNS - 1, g)
            assert steps[0] == DVE_STEPS and front_steps[0] == DVE_FRONT_STEPS

        @block.gpsimd
        def _(pool):
            tt = nc.gpsimd.tensor_tensor
            for g in range(LANES):
                nc.gpsimd.memset(probs[g][:], -1.0)
                nc.gpsimd.memset(pick[g][:], -1.0)
                nc.gpsimd.memset(xn1T[g][:], 0.0)
                last = nc.gpsimd.memset(v_tok[g][:], 1.0)
            last.then_inc(pool_set, 1)
            pool.wait_ge(dve_set, 1)

            def rstd(i, g, moments, name):
                ready(pool, i, g, moments)
                tt(rs[g][:], ve[g][:], minus_half[:, 0, :], ALU.pow).then_inc(done[name][g], 1)

            def front_rstd(i, g):
                ready(pool, i, g, "mv0")
                tt(rs_x[g][:], ve_x[g][:], minus_half[:], ALU.pow).then_inc(done["rstd0"][g], 1)

            def grow_k(i, g, l):
                half = 1 << l
                t = decay[g] if l == 0 else tot[l - 1][g]
                pair = t[:].rearrange("p (n two) -> p n two", two=2)
                if l:
                    ready(pool, i, g, "tot_level", l, LEVELS - 1)
                if l < LEVELS - 1:
                    tt(tot[l][g][:], pair[:, :, 0], pair[:, :, 1], ALU.mult).then_inc(done["tot_level"][g], 1)
                full(pool, i, g, f"level{l}")
                if l:
                    ready(pool, i, g, "kF_level", l, LEVELS)
                left = kF[g][:].rearrange("p (n two k) -> p n two k", two=2, k=half)[:, :, 0, :]
                tt(left, left, pair[:, :, 1:2].to_broadcast([P, G // (2 * half), half]), ALU.mult
                   ).then_inc(done["kF_level"][g], 1)

            def add_expert(i, g, e):
                drained(pool, i, g, f"y{e}")
                if e > 1:
                    ready(pool, i, g, "moe", e - 1, E - 1)
                tt(moe[g][:], moe[g][:], weighted[e % 2][g][:], ALU.add).then_inc(done["moe"][g], 1)

            both = range(LANES)

            def front_rk(i):
                for g in both:
                    drained(pool, i, g, "r")
                    drained(pool, i, g, "k")
                    tt(rk[g][:], r_sig[g][:], kF[g][:], ALU.mult).then_inc(done["rk"][g], 1)

            def start(i):
                for g in both:
                    drained(pool, i, g, "decay")
                    grow_k(i, g, 0)

            def main(i, next_front, last_out=True):
                for n in range(E):
                    for g in both:
                        if 0 < n < LEVELS:
                            grow_k(i, g, n)
                    for g in both:
                        if n:
                            add_expert(i, g, n)
                    for g in both:
                        if last_out and n == OUT_AT[g] + 1:
                            add_residual(i - 1, g)
                        if next_front and n == STATS_AT[g]:
                            front_rstd(i + 1, g)

            def tail_gate(i):
                for g in both:
                    ready(pool, i, g, "sig0")
                    tt(gate0[g][:], moe[g][:], sig0[g][:], ALU.mult).then_inc(done["gate0"][g], 1)
                for g in both:
                    rstd(i, g, "mv1", "rstd1")

            def tail_gate1(i):
                for g in both:
                    ready(pool, i, g, "sig1")
                    tt(gate1[g][:], sig1[g][:], f2[g][:], ALU.mult).then_inc(done["gate1"][g], 1)
                for g in both:
                    rstd(i, g, "mv2", "rstd2")

            def add_residual(i, g):
                ready(pool, i, g, "s2")
                pool.wait_ge(stored[g], 16 * i + 16)
                tt(o_out[g][:], s2[g][:], x1[g][:], ALU.add).then_inc(done["out"][g], 1)

            for g in both:
                front_rstd(0, g)
            front_rk(0)
            start(0)

            def turn(i, last_out=True):
                main(i, True, last_out)
                tail_gate(i)
                front_rk(i + 1)
                start(i + 1)
                tail_gate1(i)

            turn(0, last_out=False)
            with pool.Fori(1, TURNS - 1) as i:
                turn(i)
            main(TURNS - 1, False)
            tail_gate(TURNS - 1)
            tail_gate1(TURNS - 1)
            for g in both:
                add_residual(TURNS - 1, g)


def layout(inputs):
    f = np.float32
    a = {n: np.asarray(v) for n, v in inputs.items()}
    t = np.arange(P)
    masks = []
    for l in range(LEVELS):
        q = t[(t >> l) & 1 == 1]
        same = (t[:, None] >> (l + 1)) == (q[None, :] >> (l + 1))
        masks.append((same & ((t[:, None] >> l) & 1 == 0)).astype(f))
    return {
        "WxT": a["L0_attn_Wx"].T, "Ww": a["L0_attn_Ww"], "WvT0": a["L0_attn_Wv"].T, "Wo": a["L0_attn_Wo"],
        "Wk0": a["L0_attn_Wk"], "Wr0": a["L0_attn_Wr"],
        "routerT": a["L0_ffn_router_w"].T, "w1": a["L0_ffn_w1"],
        "w2": a["L0_ffn_w2"].reshape(E, W, P).transpose(1, 0, 2),
        "WqT": a["L1_attn_Wq"].T,
        "WkvT": np.concatenate([a["L1_attn_Wk"].T, a["L1_attn_Wv"].T], axis=1),
        "fWrT": a["L1_ffn_W_r"].T, "fWkT": a["L1_ffn_W_k"].T, "fWvT": a["L1_ffn_W_v"].T,
        "ln_g": a["L0_attn_ln_g"][:, None], "ln_b": a["L0_attn_ln_b"][:, None],
        "bw": a["L0_attn_bw"][:, None], "bq": a["L1_attn_bq"][:, None],
        "mu_r": a["L1_ffn_mu_r"][:, None], "mu_k": a["L1_ffn_mu_k"][:, None],
        "bkv": np.concatenate([a["L1_attn_bk"], a["L1_attn_bv"]])[None, :],
        "gamma": a["L1_attn_gamma"][None, :], "beta": a["L1_attn_beta"][None, :],
        "ident": np.eye(P, dtype=f), "level_mask": np.concatenate(masks, axis=1),
        "head_cols": (t[:, None] // HS == np.arange(NH)[None, :]).astype(f),
        "block_mask": (t[:, None] // AD == t[None, :] // AD).astype(f),
        "head_mask": (t[:, None] // AD == np.arange(AH)[None, :]).astype(f),
    }


def kernel(**inputs):
    import concourse.bacc as _bacc
    from concourse.bass_utils import run_bass_kernel_spmd as _run

    nc = _bacc.Bacc("TRN2", target_bir_lowering=False, num_devices=1)
    arrays = {"x": np.ascontiguousarray(inputs["L0_attn_x"])}
    for name, a in layout(inputs).items():
        arrays["in_" + name] = np.ascontiguousarray(a)
    dram = {n: nc.dram_tensor(n, a.shape, F32, kind="ExternalInput").ap() for n, a in arrays.items()}
    out = nc.dram_tensor("out", (B, T, P), F32, kind="ExternalOutput").ap()
    build(nc, dram["x"], {n[3:]: v for n, v in dram.items() if n != "x"}, out)
    r = _run(nc, [arrays], core_ids=[0])
    return r.results[0]["out"]
```

```python
from contextlib import ExitStack

import numpy as np

import concourse.bass as bass
from concourse import mybir

ALU = mybir.AluOpType
ACT = mybir.ActivationFunctionType
F32 = mybir.dt.float32
F32R = mybir.dt.float32r
U32 = mybir.dt.uint32

P = 128
B, T = 32, 256
TILES = 4
G = TILES * P
SEQ = G // T
CH = T // P
LANES = 2
TURNS = B * T // (LANES * G)
NH, HS = 2, 64
LEVELS = 7
E, W = 8, 128
AH, AD = 16, 8
EPS = 1e-5
EPS_DENOM = 1e-6

FILLS = {
    "c0": ["xnT", "decay", "r", "vw_hi", "level0", "level2", "level4", "level6", "y"],
    "c1": ["znT", "k", "route_diag", "vw_lo", "level1", "level3", "level5", "level7"],
    "h": [f"h{e}" for e in range(E)] + ["q", "kv_hi", "ffn_r", "ffn_v", "ctx_hi"],
    "y": [f"y{e}" for e in range(E)] + ["xn1T", "kv_lo", "ffn_k", "kvm", "ctx_lo"],
}
WHERE = {name: (bank, n + 1) for bank, names in FILLS.items() for n, name in enumerate(names)}

EARLY = {"WxT": P, "Ww": P, "WvT0": P, "Wo": P, "ident": P, "Wk0": P, "Wr0": P, "routerT": E,
         "head_cols": NH, "ln_g": 1, "ln_b": 1, "bw": 1, "bq": 1, "mu_r": 1, "mu_k": 1}
LATE = {"level_mask": LEVELS * HS, "w2": E * P, "WqT": P, "WkvT": 2 * P, "fWrT": P,
        "fWkT": P, "fWvT": P, "block_mask": P, "head_mask": AH}
ROWS = {"bkv": 2 * P, "gamma": P, "beta": P}

STATS_AT = (1, 3)
RSTD_AT = (2, 5)
BIAS_AT = (3, 6)
NORM_AT = (4, 7)
OUT_AT = (2, 5)
RESIDUAL_AT = (3, 7)
ACT_WEIGHS = (0, 1, 2, 3)


def passing(eng, signal, per):
    n = [0]

    def step(i, ins):
        n[0] = n[0] % per + 1
        ins.then_inc(signal, 1)
        eng.wait_ge(signal, i * per + n[0])
    return step, n


def build(nc, x, w, out):
    x_tiles = x.rearrange("b (c p) d -> p (b c) d", p=P)
    out_tiles = out.rearrange("b (c p) d -> p (b c) d", p=P)

    with ExitStack() as ctx:
        def sb(name, shape, dt=F32):
            return ctx.enter_context(nc.sbuf_tensor(name, shape, dt))

        def lanes(name, shape, dt=F32):
            return [sb(f"{name}{g}", shape, dt) for g in range(LANES)]

        def sem(name):
            return ctx.enter_context(nc.semaphore(name))

        def sems(name):
            return [sem(f"{name}{g}") for g in range(LANES)]

        def joined(name, widths):
            tile, parts, start = sb(name, [P, sum(widths.values())]), {}, 0
            for n, width in widths.items():
                parts[n] = tile[:, start:start + width]
                start += width
            return tile, parts

        early_tile, WT = joined("early", EARLY)
        late_tile, late_parts = joined("late", LATE)
        row_tile, ROW = joined("rows", ROWS)
        WT.update(late_parts)
        w2 = WT["w2"].rearrange("p (e n) -> p e n", e=E)
        vo_hi = sb("vo_hi", [P, NH * P], F32R)
        vo_lo = sb("vo_lo", [P, NH * P], F32R)
        w1_hi = sb("w1_hi", [P, E * W], F32R)
        w1_lo = sb("w1_lo", [P, E * W], F32R)
        neg_bw = sb("neg_bw", [P, 1])
        warm = sb("warm", [P, 1])
        w_decay = sb("w_decay", [P, P])
        w_vo = sb("w_vo", [P, NH * P])
        rest_r, rest_k = sb("rest_r", [P, 1]), sb("rest_k", [P, 1])
        minus_half = sb("minus_half", [P, 2, TILES])

        x_in = lanes("x_in", [P, TILES, P])
        x_res = lanes("x_res", [P, TILES, P])
        stats = lanes("stats", [P, TILES, 6])
        mv = lanes("mv", [P, TILES, 2])
        ve = lanes("ve", [P, TILES])
        rs = lanes("rs", [P, TILES])
        stats_x = lanes("stats_x", [P, TILES, 6])
        mv_x = lanes("mv_x", [P, TILES, 2])
        ve_x = lanes("ve_x", [P, 2, TILES])
        inv_x = lanes("inv_x", [P, TILES])
        rs_x = lanes("rs_x", [P, 2, TILES])
        bias_x = lanes("bias_x", [P, TILES])
        weighted = [lanes(f"weighted{n}_", [P, TILES, P]) for n in range(2)]
        xn = lanes("xn", [P, TILES, P])
        zn = lanes("zn", [P, TILES, P])
        decay = lanes("decay", [P, G])
        r_sig = lanes("r_sig", [P, G])
        kF = lanes("kF", [P, G])
        rF = lanes("rF", [P, NH, G])
        rk = lanes("rk", [P, G])
        tot = [lanes(f"tot{l}_", [P, G >> l]) for l in range(1, LEVELS)]
        a_diag = lanes("a_diag", [P, TILES, NH, P])
        a_off = lanes("a_off", [P, SEQ, NH, P])
        vw = lanes("vw", [P, TILES, NH * P])
        w1 = vw[1][:].rearrange("p j n -> p (j n)")
        probs = lanes("probs", [P, TILES, 16])
        top = lanes("top", [P, TILES, E])
        pick = lanes("pick", [P, TILES, E])
        rest = lanes("rest", [P, TILES, 16])
        den = lanes("den", [P, TILES])
        cw = lanes("cw", [P, TILES, E])
        u = lanes("u", [P, G])
        xnT = u
        xnT_hi = lanes("xnT_hi", [P, G], F32R)
        xnT_lo = lanes("xnT_lo", [P, G], F32R)
        act_sq = lanes("act_sq", [P, G])
        znT = act_sq
        znT_hi = lanes("znT_hi", [P, G], F32R)
        znT_lo = lanes("znT_lo", [P, G], F32R)
        moe = lanes("moe", [P, TILES, P])
        sig0 = lanes("sig0", [P, TILES, P])
        gate0 = lanes("gate0", [P, TILES, P])
        x1 = lanes("x1", [P, TILES, P])
        xn1 = lanes("xn1", [P, TILES, P])
        xn1T = lanes("xn1T", [P, SEQ, T + 1])
        xr = lanes("xr", [P, SEQ, T])
        xk = lanes("xk", [P, SEQ, T])
        qT = lanes("qT", [P, G])
        k_pre = weighted[0]
        k_tok = lanes("k_tok", [P, TILES, P])
        v_tok = lanes("v_tok", [P, TILES, P + 1])
        kvm = lanes("kvm", [P, SEQ, P + AH])
        rden = lanes("rden", [P, TILES, AH])
        dmax = lanes("dmax", [P, TILES, AH])
        att = lanes("att", [P, TILES, P])
        ysum = lanes("ysum", [P, TILES, P])
        centred = att
        s2 = lanes("s2", [P, TILES, P])
        gate1 = lanes("gate1", [P, TILES, P])
        r2 = lanes("r2", [P, TILES, P])
        ku = [sig0[g][:].rearrange("p j n -> p (j n)") for g in range(LANES)]
        ksq = act_sq
        f2 = lanes("f2", [P, TILES, P])
        sig1 = lanes("sig1", [P, TILES, P])
        o_out = lanes("o_out", [P, TILES, P])

        bank = {b: [ctx.enter_context(nc.psum_tensor(f"bank_{b}{g}", [P, 512], F32))
                    for g in range(LANES)] for b in FILLS}
        filled = {b: sems(f"filled_{b}") for b in FILLS}
        free = {b: sems(f"free_{b}") for b in FILLS}

        early_loaded = sem("early_loaded")
        loaded = sem("loaded")
        prep_mm = sem("prep_mm")
        prep_done = sem("prep_done")
        vo_split = sem("vo_split")
        w1_loaded = sem("w1_loaded")
        w1_split = sem("w1_split")
        dve_set = sem("dve_set")
        pool_set = sem("pool_set")
        x_loaded = sems("x_loaded")
        res_loaded = sems("res_loaded")
        stored = sems("stored")
        dve_step, dve_front_step = sem("dve_step"), sem("dve_front_step")
        dve_passed = sem("dve_passed")
        names = ["act_sq", "bias0", "cw", "gate0", "gate1", "kF_level", "k_pre", "k_tok", "ksq", "moe",
                 "mv0", "mv1", "mv2", "out", "probs", "ra", "r_head", "rF0", "rF_level", "rk", "rstd0",
                 "rstd1", "rstd2", "s2", "sig0", "sig1", "tot_level", "x1", "xk", "xn", "xnT_hi", "xnT_lo",
                 "znT_hi", "znT_lo", "xn1T", "xn1", "xr", "zn"]
        done = {n: sems(n + "_done") for n in names}

        block = ctx.enter_context(nc.Block())

        def full(eng, i, g, name):
            b, k = WHERE[name]
            eng.wait_ge(filled[b][g], i * len(FILLS[b]) + k)

        def writable(eng, i, g, name):
            b, k = WHERE[name]
            eng.wait_ge(free[b][g], i * len(FILLS[b]) + k)

        def drained(eng, i, g, name):
            b, k = WHERE[name]
            eng.wait_ge(free[b][g], i * len(FILLS[b]) + k + 1)

        def stand_alone(eng):
            eng.sem_inc(dve_passed, 1)

        def fills(ins, g, name):
            ins.then_inc(filled[WHERE[name][0]][g], 1)

        def drains(ins, g, name):
            ins.then_inc(free[WHERE[name][0]][g], 1)

        def at(name, g):
            return bank[WHERE[name][0]][g]

        def ready(eng, i, g, name, k=1, per=1):
            eng.wait_ge(done[name][g], i * per + k)


        @block.sync
        def _(sp):
            def load(i):
                for g in range(LANES):
                    tiles = x_tiles[:, bass.ds(i * (LANES * TILES) + g * TILES, TILES), :]
                    sp.dma_start(x_in[g][:], tiles).then_inc(x_loaded[g], 16)

            def load_res(i):
                for g in range(LANES):
                    tiles = x_tiles[:, bass.ds(i * (LANES * TILES) + g * TILES, TILES), :]
                    sp.dma_start(x_res[g][:], tiles).then_inc(res_loaded[g], 16)

            def store(i):
                for g in range(LANES):
                    ready(sp, i, g, "out")
                    sp.dma_start(out_tiles[:, bass.ds(i * (LANES * TILES) + g * TILES, TILES), :],
                                 o_out[g][:]).then_inc(stored[g], 16)

            def x_in_used(i):
                for g in range(LANES):
                    ready(sp, i, g, "xn")

            def x_res_used(i):
                for g in range(LANES):
                    ready(sp, i, g, "x1")

            load(0)
            sp.dma_start(early_tile[:], w["early"]).then_inc(early_loaded, 16)
            sp.dma_start(w1, w["w1"]).then_inc(w1_loaded, 16)
            sp.dma_start(late_tile[:], w["late"]).then_inc(loaded, 16)
            sp.dma_start(row_tile[:], w["rows"].to_broadcast([P, w["rows"].shape[1]])).then_inc(loaded, 16)
            load_res(0)
            x_in_used(0)
            load(1)
            with sp.Fori(1, TURNS - 1) as i:
                x_in_used(i)
                load(i + 1)
                x_res_used(i - 1)
                load_res(i)
                store(i - 1)
            x_res_used(TURNS - 2)
            load_res(TURNS - 1)
            store(TURNS - 2)
            store(TURNS - 1)
            for g in range(LANES):
                sp.wait_ge(stored[g], 16 * TURNS + 16)

        @block.tensor
        def _(pe):
            mm = nc.tensor.matmul
            pe.wait_ge(early_loaded, 16)
            mm(bank["h"][1][:, 0:P], WT["WxT"][:], WT["Ww"][:], start=True, stop=True)
            for h in range(NH):
                rows = slice(h * HS, (h + 1) * HS)
                last = mm(bank["y" if h else "h"][0][:, 0:P], WT["WvT0"][rows, :], WT["Wo"][rows, :],
                          start=True, stop=True)
            last.then_inc(prep_mm, 1)

            def transposes(i, g, name, src):
                writable(pe, i, g, name)
                for j in range(TILES):
                    last = nc.tensor.transpose(at(name, g)[:, j * P:(j + 1) * P], src[:, j, :], WT["ident"][:])
                fills(last, g, name)

            def product(i, g, name, weight, moving):
                writable(pe, i, g, name)
                fills(mm(at(name, g)[:], weight, moving, start=True, stop=True), g, name)

            def token_product(i, g, name, tokT, weight, tiles, step):
                writable(pe, i, g, name)
                n = weight.shape[1]
                for m, j in enumerate(tiles):
                    last = mm(at(name, g)[:, m * step:m * step + n], tokT[:, j * P:(j + 1) * P], weight,
                              start=True, stop=True)
                fills(last, g, name)

            def route_diag(i, g):
                writable(pe, i, g, "route_diag")
                ps = at("route_diag", g)
                for j in range(TILES):
                    mm(ps[:, j * E:(j + 1) * E], xnT[g][:, j * P:(j + 1) * P], WT["routerT"][:],
                       start=True, stop=True)
                ready(pe, i, g, "rk")
                for j in range(TILES):
                    last = mm(ps[:, 64 + j * NH:64 + (j + 1) * NH], rk[g][:, j * P:(j + 1) * P],
                              WT["head_cols"][:], start=True, stop=True)
                fills(last, g, "route_diag")

            def level(i, g, l):
                name = f"level{l}"
                if l == 0:
                    drained(pe, i, g, "k")
                    ready(pe, i, g, "rF0")
                else:
                    ready(pe, i, g, "kF_level", l, LEVELS)
                    ready(pe, i, g, "rF_level", l, LEVELS)
                writable(pe, i, g, name)
                ps = at(name, g)
                if l < LEVELS:
                    half = 1 << l
                    for j in range(TILES):
                        q = rF[g][:, :, j * P:(j + 1) * P].rearrange("p h (n two k) -> p h n two k",
                                                                     two=2, k=half)[:, :, :, 1, :]
                        last = mm(ps[:, j * P:(j + 1) * P], kF[g][:, j * P:(j + 1) * P], q,
                                  start=True, stop=True)
                else:
                    for s in range(SEQ):
                        j = s * CH
                        last = mm(ps[:, s * NH * P:(s + 1) * NH * P], kF[g][:, j * P:(j + 1) * P],
                                  rF[g][:, :, (j + 1) * P:(j + 2) * P], start=True, stop=True)
                fills(last, g, name)

            def expert_in(i, g, e):
                name, cols = f"h{e}", slice(e * W, (e + 1) * W)
                writable(pe, i, g, name)
                o = at(name, g)[:]
                mm(o, w1_hi[:, cols], xnT_hi[g][:], start=True, stop=False)
                mm(o, w1_lo[:, cols], xnT_hi[g][:], start=False, stop=False)
                fills(mm(o, w1_hi[:, cols], xnT_lo[g][:], start=False, stop=True), g, name)

            def expert_out(i, g, e):
                name = f"y{e}"
                writable(pe, i, g, name)
                ready(pe, i, g, "act_sq", e + 1, E)
                for j in range(TILES):
                    last = mm(at(name, g)[:, j * P:(j + 1) * P], act_sq[g][:, j * P:(j + 1) * P],
                              w2[:, e, :], start=True, stop=True)
                fills(last, g, name)

            def mix(i, g):
                writable(pe, i, g, "y")
                drained(pe, i, g, "level7")
                for j in range(TILES):
                    o = at("y", g)[:, j * P:(j + 1) * P]
                    parts = [(a_diag[g][:, j, h, :], vw[g][:, j, h * P:(h + 1) * P]) for h in range(NH)]
                    if j % CH:
                        parts += [(a_off[g][:, j // CH, h, :], vw[g][:, j - 1, h * P:(h + 1) * P])
                                  for h in range(NH)]
                    for n, (s, v) in enumerate(parts):
                        last = mm(o, s, v, start=(n == 0), stop=(n == len(parts) - 1))
                fills(last, g, "y")

            def kv_sums(i, g):
                writable(pe, i, g, "kvm")
                ready(pe, i, g, "k_tok", 2, 2)
                drained(pe, i, g, "kv_hi")
                for s in range(SEQ):
                    for c in range(CH):
                        j = s * CH + c
                        last = mm(at("kvm", g)[:, s * 256:s * 256 + P + 1], k_tok[g][:, j, :],
                                  v_tok[g][:, j, :], start=(c == 0), stop=(c == CH - 1))
                fills(last, g, "kvm")

            def context(i, g, name, tiles):
                writable(pe, i, g, name)
                drained(pe, i, g, "q")
                drained(pe, i, g, "kvm")
                for m, j in enumerate(tiles):
                    last = mm(at(name, g)[:, m * 256:m * 256 + P + AH], qT[g][:, j * P:(j + 1) * P],
                              kvm[g][:, j // CH, :], start=True, stop=True)
                fills(last, g, name)

            both = range(LANES)

            def front_first(i, prepared=None):
                for g in both:
                    ready(pe, i, g, "xn")
                    transposes(i, g, "xnT", xn[g])
                    ready(pe, i, g, "zn")
                    transposes(i, g, "znT", zn[g])
                if prepared:
                    pe.wait_ge(*prepared)
                for g in both:
                    drained(pe, i, g, "znT")
                    product(i, g, "decay", w_decay[:], znT[g][:])
                    product(i, g, "k", WT["Wk0"][:], znT[g][:])
                for g in both:
                    product(i, g, "r", WT["Wr0"][:], znT[g][:])

            def front_values(i):
                for g in both:
                    ready(pe, i, g, "znT_hi")
                    ready(pe, i, g, "znT_lo")
                    for m, name in enumerate(("vw_lo", "vw_hi")):
                        writable(pe, i, g, name)
                        for n in range(2):
                            o = at(name, g)[:, n * NH * P:(n + 1) * NH * P]
                            tokens = slice((2 * m + n) * P, (2 * m + n + 1) * P)
                            mm(o, znT_hi[g][:, tokens], vo_hi[:], start=True, stop=False)
                            mm(o, znT_hi[g][:, tokens], vo_lo[:], start=False, stop=False)
                            last = mm(o, znT_lo[g][:, tokens], vo_hi[:], start=False, stop=True)
                        fills(last, g, name)

            def front_route(i, g):
                drained(pe, i, g, "xnT")
                route_diag(i, g)

            def front_level(i):
                for g in both:
                    level(i, g, 0)

            def main(i):
                for g in both:
                    level(i, g, 1)
                    ready(pe, i, g, "xnT_hi")
                    ready(pe, i, g, "xnT_lo")
                    expert_in(i, g, 0)
                for n in range(E):
                    for g in both:
                        l = n if g and n == LEVELS else n + 1
                        if n and l <= LEVELS and not (g and n + 1 == LEVELS):
                            level(i, g, l)
                    for g in both:
                        expert_out(i, g, n)
                    if n + 1 < E:
                        for g in both:
                            expert_in(i, g, n + 1)
                for g in both:
                    mix(i, g)

            def tail_start(i):
                for g in both:
                    ready(pe, i, g, "xn1")
                    transposes(i, g, "xn1T", xn1[g])
                for g in both:
                    ready(pe, i, g, "xn1T")
                    writable(pe, i, g, "q")
                    fills(mm(at("q", g)[:], WT["WqT"][:], xn1T[g][:, :, 1:], start=True, stop=True), g, "q")
                for g in both:
                    for name, tiles in (("kv_lo", (0, 1)), ("kv_hi", (2, 3))):
                        writable(pe, i, g, name)
                        for m, j in enumerate(tiles):
                            c = 1 + (j % CH) * P
                            last = mm(at(name, g)[:, m * 256:(m + 1) * 256], xn1T[g][:, j // CH, c:c + P],
                                      WT["WkvT"][:], start=True, stop=True)
                        fills(last, g, name)

            def tail_ffn(i, g):
                ready(pe, i, g, "xk")
                product(i, g, "ffn_k", WT["fWkT"][:], xk[g][:].rearrange("p s t -> p (s t)"))
                ready(pe, i, g, "xr")
                token_product(i, g, "ffn_r", xr[g][:].rearrange("p s t -> p (s t)"), WT["fWrT"][:],
                              range(TILES), P)

            def tail_sums(i):
                for g in both:
                    kv_sums(i, g)

            def tail_end(i):
                for g in both:
                    ready(pe, i, g, "ksq")
                    token_product(i, g, "ffn_v", ksq[g], WT["fWvT"][:], range(TILES), P)
                for g in both:
                    context(i, g, "ctx_lo", (0, 1))
                    context(i, g, "ctx_hi", (2, 3))

            front_first(0, prepared=(prep_done, 4))
            for g in both:
                front_route(0, g)
            pe.wait_ge(vo_split, 2)
            front_values(0)
            pe.wait_ge(dve_set, 3)
            pe.wait_ge(pool_set, 1)
            front_level(0)
            pe.wait_ge(w1_split, 2)

            def turn(i):
                main(i)
                front_first(i + 1)
                tail_start(i)
                for g in both:
                    front_route(i + 1, g)
                    tail_ffn(i, g)
                front_values(i + 1)
                tail_sums(i)
                front_level(i + 1)
                tail_end(i)

            turn(0)
            with pe.Fori(1, TURNS - 1) as i:
                turn(i)
            main(TURNS - 1)
            tail_start(TURNS - 1)
            for g in both:
                tail_ffn(TURNS - 1, g)
            tail_sums(TURNS - 1)
            tail_end(TURNS - 1)

        @block.scalar
        def _(act):
            af = nc.scalar.activation
            act.wait_ge(dve_set, 1)
            af(warm[:], minus_half[:, 0, 0:1], ACT.Sigmoid)

            def drain(i, g, name, o, func, **kw):
                full(act, i, g, name)
                drains(af(o, at(name, g)[:], func, **kw), g, name)

            def expert_act(i, g, e):
                drain(i, g, f"h{e}", u[g][:], ACT.Relu)
                drained(act, i, g, f"h{e}")
                if e:
                    b, k = WHERE[f"y{e - 1}"]
                    act.wait_ge(filled[b][g], i * len(FILLS[b]) + k)
                af(act_sq[g][:], u[g][:], ACT.Square).then_inc(done["act_sq"][g], 1)

            def weigh(i, g, e):
                full(act, i, g, f"y{e}")
                if e == ACT_WEIGHS[0]:
                    ready(act, i, g, "cw")
                if e > 2:
                    ready(act, i, g, "moe", e - 2, E - 1)
                o = weighted[e % 2][g] if e else moe[g]
                for j in range(TILES):
                    last = af(o[:, j, :], at(f"y{e}", g)[:, j * P:(j + 1) * P], ACT.Copy,
                              scale=cw[g][:, j, e:e + 1])
                drains(last, g, f"y{e}")

            both = range(LANES)

            def front_norm(i, g):
                ready(act, i, g, "bias0")
                for j in range(TILES):
                    last = af(xn[g][:, j, :], x_in[g][:, j, :], ACT.Identity, scale=rs_x[g][:, 0, j:j + 1],
                              bias=bias_x[g][:, j:j + 1])
                last.then_inc(done["xn"][g], 1)
                ready(act, i, g, "xn")
                for j in range(TILES):
                    last = af(zn[g][:, j, :], xn[g][:, j, :], ACT.Copy, scale=rs_x[g][:, 1, j:j + 1])
                last.then_inc(done["zn"][g], 1)

            def front_first(i):
                for g in both:
                    drain(i, g, "xnT", xnT[g][:], ACT.Copy)
                    drain(i, g, "znT", znT[g][:], ACT.Identity, bias=WT["ln_b"][:], scale=WT["ln_g"][:])
                for g in both:
                    drain(i, g, "decay", decay[g][:], ACT.Sigmoid, bias=neg_bw[:], scale=-1.0)
                    drain(i, g, "k", kF[g][:], ACT.Copy)
                for g in both:
                    drain(i, g, "r", r_sig[g][:], ACT.Sigmoid)

            def front_hi(i):
                for g in both:
                    drained(act, i, g, "xnT")
                    af(xnT_hi[g][:], xnT[g][:], ACT.Copy).then_inc(done["xnT_hi"][g], 1)
                for g in both:
                    drained(act, i, g, "znT")
                    af(znT_hi[g][:], znT[g][:], ACT.Copy).then_inc(done["znT_hi"][g], 1)

            def front_values(i):
                for g in both:
                    drain(i, g, "vw_lo", vw[g][:, 0:2, :].rearrange("p j n -> p (j n)"), ACT.Copy)
                    drain(i, g, "vw_hi", vw[g][:, 2:4, :].rearrange("p j n -> p (j n)"), ACT.Copy)

            def front_route(i, g):
                full(act, i, g, "route_diag")
                af(probs[g][:, :, 0:E], at("route_diag", g)[:, 0:TILES * E].rearrange(
                    "p (j e) -> p j e", e=E), ACT.Sigmoid).then_inc(done["probs"][g], 1)

            def main(i, next_front):
                for e in range(E):
                    if e == LEVELS:
                        drain(i, 0, "level7", a_off[0][:].rearrange("p s h t -> p (s h t)"), ACT.Copy)
                    for g in both:
                        expert_act(i, g, e)
                    if e == LEVELS:
                        drain(i, 1, "level7", a_off[1][:].rearrange("p s h t -> p (s h t)"), ACT.Copy)
                    for g in both:
                        if e in ACT_WEIGHS:
                            weigh(i, g, e)
                    for g in both:
                        if e == NORM_AT[g] and next_front:
                            front_norm(i + 1, g)
                for g in both:
                    ready(act, i, g, "moe", E - 1, E - 1)
                    af(sig0[g][:], moe[g][:], ACT.Sigmoid).then_inc(done["sig0"][g], 1)

            def tail_start(i, next_front):
                for g in both:
                    full(act, i, g, "xn1T")
                    now = at("xn1T", g)[:].rearrange("p (s t) -> p s t", s=SEQ)
                    af(xn1T[g][:, :, 1:], now, ACT.Copy).then_inc(done["xn1T"][g], 1)
                for g in both:
                    now = at("xn1T", g)[:].rearrange("p (s t) -> p s t", s=SEQ)
                    af(xk[g][:], now, ACT.Copy, scale=WT["mu_k"][:])
                    drains(af(xr[g][:], now, ACT.Copy, scale=WT["mu_r"][:]), g, "xn1T")
                    drain(i, g, "q", qT[g][:], ACT.Relu, bias=WT["bq"][:])
                if next_front:
                    front_hi(i + 1)
                for g in both:
                    for m in range(2):
                        ready(act, i, g, "k_pre", m + 1, 2)
                        af(k_tok[g][:, 2 * m:2 * m + 2, :], k_pre[g][:, 2 * m:2 * m + 2, :], ACT.Relu
                           ).then_inc(done["k_tok"][g], 1)

            def tail_ffn(i, g, next_front):
                drain(i, g, "ffn_k", ku[g][:], ACT.Relu)
                drained(act, i, g, "ffn_k")
                if next_front:
                    ready(act, i + 1, g, "znT_lo")
                af(ksq[g][:], ku[g][:], ACT.Square).then_inc(done["ksq"][g], 1)
                drain(i, g, "ffn_r", r2[g][:].rearrange("p j n -> p (j n)"), ACT.Sigmoid)

            def tail_end(i):
                for g in both:
                    drained(act, i, g, "ffn_v")
                    af(sig1[g][:], f2[g][:], ACT.Sigmoid).then_inc(done["sig1"][g], 1)

            for g in both:
                front_norm(0, g)
            act.wait_ge(early_loaded, 16)
            nc.scalar.mul(neg_bw[:], WT["bw"][:], -1.0).then_inc(prep_done, 1)
            act.wait_ge(prep_mm, 1)
            nc.scalar.copy(w_decay[:], bank["h"][1][:, 0:P]).then_inc(prep_done, 1)
            nc.scalar.copy(w_vo[:, 0:P], bank["h"][0][:, 0:P]).then_inc(prep_done, 1)
            nc.scalar.copy(w_vo[:, P:2 * P], bank["y"][0][:, 0:P]).then_inc(prep_done, 1)
            act.wait_ge(prep_done, 4)
            front_first(0)
            front_hi(0)
            act.wait_ge(pool_set, 1)
            for g in both:
                front_route(0, g)
            act.wait_ge(w1_split, 2)
            front_values(0)
            act.wait_ge(loaded, 32)

            def turn(i):
                main(i, True)
                front_first(i + 1)
                tail_start(i, True)
                for g in both:
                    front_route(i + 1, g)
                    tail_ffn(i, g, True)
                front_values(i + 1)
                tail_end(i)

            turn(0)
            with act.Fori(1, TURNS - 1) as i:
                turn(i)
            main(TURNS - 1, False)
            tail_start(TURNS - 1, False)
            for g in both:
                tail_ffn(TURNS - 1, g, False)
            tail_end(TURNS - 1)

        DVE_STEPS, DVE_FRONT_STEPS = LANES * 9, LANES * 9

        @block.vector
        def _(dve):
            tt, ts, stt = nc.vector.tensor_tensor, nc.vector.tensor_scalar, nc.vector.scalar_tensor_tensor
            nc.vector.memset(minus_half[:], -0.5).then_inc(dve_set, 1)
            for g in range(LANES):
                dve.sem_inc(free["c0"][g], 1)
                dve.sem_inc(free["c1"][g], 1)
                dve.sem_inc(stored[g], 16)
            step, steps = passing(dve, dve_step, DVE_STEPS)
            front_step, front_steps = passing(dve, dve_front_step, DVE_FRONT_STEPS)

            def moments(i, g, src, st, out, passed_on):
                for j in range(TILES):
                    last = nc.vector.bn_stats(st[g][:, j, :], src[:, j, :])
                passed_on(i, last)
                stand_alone(dve)
                for j in range(TILES):
                    last = nc.vector.bn_aggr(out[g][:, j, :], st[g][:, j, :])
                passed_on(i, last)

            def tail_moments(i, g, src, name):
                moments(i, g, src, stats, mv, step)
                ts(ve[g][:], mv[g][:, :, 1], EPS, None, ALU.add).then_inc(done[name][g], 1)

            def normalise(i, g, o, src, mean, scale, name):
                for j in range(TILES):
                    last = ts(o[:, j, :], src[:, j, :], mean[:, j:j + 1], scale[:, j:j + 1],
                              ALU.subtract, ALU.mult)
                last.then_inc(done[name][g], 1)

            def level_scores(i, g, l):
                half = 1 << l
                full(dve, i, g, f"level{l}")
                drained(dve, i, g, f"level{l - 1}" if l else "route_diag")
                o = a_diag[g][:].rearrange("p j h (n two k) -> p (j h) n two k", two=2, k=half)[:, :, :, 1, :]
                ps = at(f"level{l}", g)[:].rearrange("p (m n k) -> p m n k", m=TILES * NH, k=half)
                m = WT["level_mask"][:, l * HS:(l + 1) * HS].bitcast(U32).rearrange(
                    "p (n k) -> p n k", k=half).unsqueeze(1).to_broadcast([P, TILES * NH, HS // half, half])
                stand_alone(dve)
                ins = nc.vector.copy_predicated(o, m, ps)
                drains(ins, g, f"level{l}")

            def grow_r(i, g, l):
                half = 1 << l
                full(dve, i, g, f"level{l}")
                if l:
                    ready(dve, i, g, "tot_level", l, LEVELS - 1)
                    dve.wait_ge(done["rF_level"][g], i * LEVELS + l)
                t = decay[g] if l == 0 else tot[l - 1][g]
                right = rF[g][:].rearrange("p h (n two k) -> p h n two k", two=2, k=half)[:, :, :, 1, :]
                left_tot = t[:].rearrange("p (n two) -> p n two", two=2)[:, :, 0:1]
                left_tot = left_tot.unsqueeze(1).to_broadcast([P, NH, G // (2 * half), half])
                tt(right, right, left_tot, ALU.mult).then_inc(done["rF_level"][g], 1)

            def weigh(i, g, e):
                full(dve, i, g, f"y{e}")
                if e > 2:
                    ready(dve, i, g, "moe", e - 2, E - 1)
                o = weighted[e % 2][g] if e else moe[g]
                drains(tt(o[:], at(f"y{e}", g)[:].rearrange("p (j n) -> p j n", j=TILES),
                          cw[g][:, :, e:e + 1].to_broadcast([P, TILES, P]), ALU.mult), g, f"y{e}")

            def route(i, g):
                ready(dve, i, g, "probs")
                stand_alone(dve)
                for j in range(TILES):
                    last = nc.vector.max(top[g][:, j, :], probs[g][:, j, 0:E])
                front_step(i, last)
                nc.vector.tensor_copy(pick[g][:, :, 0:2], top[g][:, :, 0:2])
                front_step(i, tt(den[g][:], top[g][:, :, 0], top[g][:, :, 1], ALU.add))
                ts(den[g][:], den[g][:], 1e-20, None, ALU.add)
                for j in range(TILES):
                    last = nc.vector.match_replace(rest[g][:, j, :], pick[g][:, j, :], probs[g][:, j, :], 0.0)
                front_step(i, last)
                nc.vector.reciprocal(den[g][:], den[g][:])
                front_step(i, tt(cw[g][:], probs[g][:, :, 0:E], rest[g][:, :, 0:E], ALU.subtract))
                tt(cw[g][:], cw[g][:], den[g][:].unsqueeze(2).to_broadcast([P, TILES, E]), ALU.mult
                   ).then_inc(done["cw"][g], 1)
                ready(dve, i, g, "cw")

            both = range(LANES)

            def front_stats(i, g):
                dve.wait_ge(x_loaded[g], 16 * i + 16)
                moments(i, g, x_in[g], stats_x, mv_x, front_step)
                var = mv_x[g][:, :, 1]
                front_step(i, ts(ve_x[g][:, 0, :], var, EPS, None, ALU.add))
                front_step(i, nc.vector.reciprocal(inv_x[g][:], ve_x[g][:, 0, :]))
                front_step(i, tt(inv_x[g][:], inv_x[g][:], var, ALU.mult))
                ts(ve_x[g][:, 1, :], inv_x[g][:], EPS, None, ALU.add).then_inc(done["mv0"][g], 1)

            def front_bias(i, g):
                ready(dve, i, g, "rstd0")
                stt(bias_x[g][:], mv_x[g][:, :, 0], -1.0, rs_x[g][:, 0, :], ALU.mult, ALU.mult
                    ).then_inc(done["bias0"][g], 1)

            def front_diag(i):
                for g in both:
                    full(dve, i, g, "route_diag")
                    ready(dve, i, g, "probs")
                    d = at("route_diag", g)[:, 64:64 + TILES * NH].unsqueeze(2).to_broadcast([P, TILES * NH, P])
                    m = WT["ident"][:].bitcast(U32).unsqueeze(1).to_broadcast([P, TILES * NH, P])
                    stand_alone(dve)
                    ins = nc.vector.copy_predicated(a_diag[g][:].rearrange("p j h t -> p (j h) t"), m, d)
                    drains(ins, g, "route_diag")

            def front_route(i):
                for g in both:
                    route(i, g)

            def start(i):
                for g in both:
                    ready(dve, i, g, "rF0")
                    grow_r(i, g, 0)
                    level_scores(i, g, 0)

            def inner_level(i, l):
                for g in both:
                    grow_r(i, g, l)
                    level_scores(i, g, l)

            def main(i, next_front, last_out=True):
                for n in range(E):
                    if 0 < n and n + 1 < LEVELS:
                        inner_level(i, n + 1)
                    for g in both:
                        if n not in ACT_WEIGHS:
                            weigh(i, g, n)
                    for g in both:
                        if last_out and n == OUT_AT[g]:
                            tail_out(i - 1, g)
                        if next_front and n == STATS_AT[g]:
                            front_stats(i + 1, g)
                        if next_front and n == BIAS_AT[g]:
                            front_bias(i + 1, g)

            def tail_x1(i):
                for g in both:
                    ready(dve, i, g, "gate0")
                    full(dve, i, g, "y")
                    drains(tt(x1[g][:].rearrange("p j n -> p (j n)"), at("y", g)[:],
                              gate0[g][:].rearrange("p j n -> p (j n)"), ALU.mult), g, "y")
                for g in both:
                    drained(dve, i, g, "y")
                    dve.wait_ge(res_loaded[g], 16 * i + 16)
                    tt(x1[g][:], x1[g][:], x_res[g][:], ALU.add).then_inc(done["x1"][g], 1)
                    ready(dve, i, g, "x1")
                    tail_moments(i, g, x1[g], "mv1")

            def tail_xn1(i):
                for g in both:
                    ready(dve, i, g, "rstd1")
                    normalise(i, g, xn1[g], x1[g], mv[g][:, :, 0], rs[g][:], "xn1")

            def tail_shift(i, g):
                drained(dve, i, g, "xn1T")
                prev = xn1T[g][:, :, 0:T]
                stt(xk[g][:], prev, rest_k[:], xk[g][:], ALU.mult, ALU.add).then_inc(done["xk"][g], 1)
                stt(xr[g][:], prev, rest_r[:], xr[g][:], ALU.mult, ALU.add).then_inc(done["xr"][g], 1)

            def tail_kv(i, g):
                for m, name in enumerate(("kv_lo", "kv_hi")):
                    full(dve, i, g, name)
                    ps = at(name, g)[:].rearrange("p (j n) -> p j n", n=2 * P)
                    js = slice(2 * m, 2 * m + 2)
                    tt(k_pre[g][:, js, :], ps[:, :, 0:P],
                       ROW["bkv"][:, 0:P].unsqueeze(1).to_broadcast([P, 2, P]), ALU.add
                       ).then_inc(done["k_pre"][g], 1)
                    drains(tt(v_tok[g][:, js, 0:P], ps[:, :, P:2 * P],
                              ROW["bkv"][:, P:2 * P].unsqueeze(1).to_broadcast([P, 2, P]), ALU.add),
                           g, name)

            def tail_kvm(i):
                for g in both:
                    full(dve, i, g, "kvm")
                    ps = at("kvm", g)[:].rearrange("p (s n) -> p s n", n=256)
                    tt(kvm[g][:, :, 0:P], ps[:, :, 0:P],
                       WT["block_mask"][:].unsqueeze(1).to_broadcast([P, SEQ, P]), ALU.mult)
                    drains(tt(kvm[g][:, :, P:], ps[:, :, P:P + 1].to_broadcast([P, SEQ, AH]),
                              WT["head_mask"][:].unsqueeze(1).to_broadcast([P, SEQ, AH]), ALU.mult), g, "kvm")

            def tail_f2(i):
                for g in both:
                    full(dve, i, g, "ffn_v")
                    drained(dve, i, g, "ffn_r")
                    drains(tt(f2[g][:].rearrange("p j n -> p (j n)"), at("ffn_v", g)[:],
                              r2[g][:].rearrange("p j n -> p (j n)"), ALU.mult), g, "ffn_v")

            def tail_ctx(i):
                for g in both:
                    halves = [(name, slice(2 * m, 2 * m + 2), at(name, g)[:].rearrange("p (j n) -> p j n", n=256))
                              for m, name in enumerate(("ctx_lo", "ctx_hi"))]
                    for name, js, ps in halves:
                        full(dve, i, g, name)
                        last = ts(dmax[g][:, js, :], ps[:, :, P:P + AH], EPS_DENOM, None, ALU.max)
                    step(i, last)
                    step(i, nc.vector.reciprocal(rden[g][:], dmax[g][:]))
                    for name, js, ps in halves:
                        drains(tt(att[g][:, js, :].rearrange("p j (h d) -> p j h d", d=AD),
                                  ps[:, :, 0:P].rearrange("p j (h d) -> p j h d", d=AD),
                                  rden[g][:, js, :].unsqueeze(3).to_broadcast([P, 2, AH, AD]), ALU.mult),
                               g, name)

            def tail_sum(i):
                for g in both:
                    drained(dve, i, g, "ctx_lo")
                    drained(dve, i, g, "ctx_hi")
                    step(i, tt(ysum[g][:], att[g][:], xn1[g][:], ALU.add))
                    tail_moments(i, g, ysum[g], "mv2")

            def tail_out(i, g):
                ready(dve, i, g, "rstd2")
                for j in range(TILES):
                    last = stt(centred[g][:, j, :], ysum[g][:, j, :], mv[g][:, j, 0:1], ROW["gamma"][:],
                               ALU.subtract, ALU.mult)
                step(i, last)
                for j in range(TILES):
                    last = stt(s2[g][:, j, :], centred[g][:, j, :], rs[g][:, j:j + 1], ROW["beta"][:],
                               ALU.mult, ALU.add)
                step(i, last)
                ready(dve, i, g, "gate1")
                tt(s2[g][:], s2[g][:], gate1[g][:], ALU.mult).then_inc(done["s2"][g], 1)

            for g in both:
                front_stats(0, g)
            for g in both:
                front_bias(0, g)
            for g in both:
                last = nc.vector.memset(a_diag[g][:], 0.0)
            last.then_inc(dve_set, 1)
            dve.wait_ge(prep_done, 4)
            for g in both:
                dve.sem_inc(free["h"][g], 1)
                dve.sem_inc(free["y"][g], 1)
            nc.vector.tensor_copy(vo_hi[:], w_vo[:]).then_inc(vo_split, 1)
            dve.wait_ge(vo_split, 1)
            tt(vo_lo[:], w_vo[:], vo_hi[:].bitcast(F32), ALU.subtract).then_inc(vo_split, 1)
            dve.wait_ge(w1_loaded, 16)
            nc.vector.tensor_copy(w1_hi[:], w1).then_inc(w1_split, 1)
            dve.wait_ge(dve_set, 2)
            dve.wait_ge(pool_set, 1)
            dve.wait_ge(early_loaded, 16)
            ts(rest_k[:], WT["mu_k"][:], -1.0, 1.0, ALU.mult, ALU.add)
            ts(rest_r[:], WT["mu_r"][:], -1.0, 1.0, ALU.mult, ALU.add).then_inc(dve_set, 1)
            dve.wait_ge(dve_set, 3)
            for g in both:
                drained(dve, 0, g, "r")
                drained(dve, 0, g, "decay")
                for h in range(NH):
                    last = stt(rF[g][:, h, :], r_sig[g][:], WT["head_cols"][:, h:h + 1], decay[g][:],
                               ALU.mult, ALU.mult)
                last.then_inc(done["rF0"][g], 1)
            front_diag(0)
            front_route(0)
            dve.wait_ge(loaded, 32)
            start(0)
            inner_level(0, 1)

            def turn(i, last_out=True):
                main(i, True, last_out)
                tail_x1(i)
                tail_xn1(i)
                for g in both:
                    tail_shift(i, g)
                for g in both:
                    tail_kv(i, g)
                front_diag(i + 1)
                front_route(i + 1)
                tail_kvm(i)
                start(i + 1)
                tail_f2(i)
                tail_ctx(i)
                inner_level(i + 1, 1)
                tail_sum(i)

            turn(0, last_out=False)
            with dve.Fori(1, TURNS - 1) as i:
                turn(i)
            main(TURNS - 1, False)
            tail_x1(TURNS - 1)
            tail_xn1(TURNS - 1)
            for g in both:
                tail_shift(TURNS - 1, g)
            for g in both:
                tail_kv(TURNS - 1, g)
            tail_kvm(TURNS - 1)
            tail_f2(TURNS - 1)
            tail_ctx(TURNS - 1)
            tail_sum(TURNS - 1)
            for g in both:
                tail_out(TURNS - 1, g)
            assert steps[0] == DVE_STEPS and front_steps[0] == DVE_FRONT_STEPS

        @block.gpsimd
        def _(pool):
            tt = nc.gpsimd.tensor_tensor
            for g in range(LANES):
                nc.gpsimd.memset(probs[g][:], -1.0)
                nc.gpsimd.memset(pick[g][:], -1.0)
                nc.gpsimd.memset(xn1T[g][:], 0.0)
                last = nc.gpsimd.memset(v_tok[g][:], 1.0)
            last.then_inc(pool_set, 1)
            pool.wait_ge(dve_set, 1)
            pool.wait_ge(early_loaded, 16)

            both = range(LANES)

            def rstd(i, g, moments, name):
                ready(pool, i, g, moments)
                tt(rs[g][:], ve[g][:], minus_half[:, 0, :], ALU.pow).then_inc(done[name][g], 1)

            def front_rstd(i, g):
                ready(pool, i, g, "mv0")
                tt(rs_x[g][:], ve_x[g][:], minus_half[:], ALU.pow).then_inc(done["rstd0"][g], 1)

            def pairs(g, l):
                t = decay[g] if l == 0 else tot[l - 1][g]
                return t[:].rearrange("p (n two) -> p n two", two=2)

            def totals(i, l):
                for g in both:
                    if l:
                        ready(pool, i, g, "tot_level", l, LEVELS - 1)
                    tt(tot[l][g][:], pairs(g, l)[:, :, 0], pairs(g, l)[:, :, 1], ALU.mult
                       ).then_inc(done["tot_level"][g], 1)

            def grow_k(i, l):
                half = 1 << l
                for g in both:
                    full(pool, i, g, f"level{l}")
                    if l:
                        ready(pool, i, g, "tot_level", l, LEVELS - 1)
                        ready(pool, i, g, "kF_level", l, LEVELS)
                    left = kF[g][:].rearrange("p (n two k) -> p n two k", two=2, k=half)[:, :, 0, :]
                    tt(left, left, pairs(g, l)[:, :, 1:2].to_broadcast([P, G // (2 * half), half]), ALU.mult
                       ).then_inc(done["kF_level"][g], 1)

            def inner_level(i, l):
                grow_k(i, l)
                if l < LEVELS - 1:
                    totals(i, l)

            def add_expert(i, g, e):
                drained(pool, i, g, f"y{e}")
                if e > 1:
                    ready(pool, i, g, "moe", e - 1, E - 1)
                tt(moe[g][:], moe[g][:], weighted[e % 2][g][:], ALU.add).then_inc(done["moe"][g], 1)

            def front_rk(i):
                for g in both:
                    drained(pool, i, g, "r")
                    drained(pool, i, g, "k")
                    drained(pool, i, g, "decay")
                    tt(rk[g][:], r_sig[g][:], kF[g][:], ALU.mult).then_inc(done["rk"][g], 1)

            def front_r(i):
                for g in both:
                    tt(rF[g][:, 0, :], r_sig[g][:], decay[g][:], ALU.mult).then_inc(done["ra"][g], 1)
                for g in both:
                    pool.wait_ge(done["ra"][g], i)
                    own = [WT["head_cols"][:, h:h + 1].to_broadcast([P, G]) for h in range(NH)]
                    tt(rF[g][:, 1, :], rF[g][:, 0, :], own[1], ALU.mult).then_inc(done["r_head"][g], 1)
                    pool.wait_ge(done["r_head"][g], i)
                    tt(rF[g][:, 0, :], rF[g][:, 0, :], own[0], ALU.mult).then_inc(done["rF0"][g], 1)

            def front_zn_lo(i):
                for g in both:
                    ready(pool, i, g, "znT_hi")
                    tt(znT_lo[g][:], znT[g][:], znT_hi[g][:].bitcast(F32), ALU.subtract
                       ).then_inc(done["znT_lo"][g], 1)

            def front_lo(i):
                for g in both:
                    ready(pool, i, g, "xnT_hi")
                    tt(xnT_lo[g][:], xnT[g][:], xnT_hi[g][:].bitcast(F32), ALU.subtract
                       ).then_inc(done["xnT_lo"][g], 1)

            def start(i):
                for g in both:
                    drained(pool, i, g, "decay")
                totals(i, 0)
                grow_k(i, 0)

            def main(i, next_front, last_out=True):
                for n in range(E):
                    if 0 < n and n + 1 < LEVELS:
                        inner_level(i, n + 1)
                    for g in both:
                        if last_out and n == RESIDUAL_AT[g]:
                            add_residual(i - 1, g)
                    for g in both:
                        if n:
                            add_expert(i, g, n)
                    for g in both:
                        if next_front and n == RSTD_AT[g]:
                            front_rstd(i + 1, g)

            def tail_gate(i):
                for g in both:
                    ready(pool, i, g, "sig0")
                    tt(gate0[g][:], moe[g][:], sig0[g][:], ALU.mult).then_inc(done["gate0"][g], 1)
                for g in both:
                    rstd(i, g, "mv1", "rstd1")

            def tail_gate1(i):
                for g in both:
                    ready(pool, i, g, "sig1")
                    tt(gate1[g][:], sig1[g][:], f2[g][:], ALU.mult).then_inc(done["gate1"][g], 1)

            def tail_rstd2(i):
                for g in both:
                    rstd(i, g, "mv2", "rstd2")


            def add_residual(i, g):
                ready(pool, i, g, "s2")
                pool.wait_ge(stored[g], 16 * i + 16)
                tt(o_out[g][:], s2[g][:], x1[g][:], ALU.add).then_inc(done["out"][g], 1)

            for g in both:
                front_rstd(0, g)
            pool.wait_ge(w1_split, 1)
            tt(w1_lo[:], w1, w1_hi[:].bitcast(F32), ALU.subtract).then_inc(w1_split, 1)
            front_rk(0)
            front_zn_lo(0)
            front_lo(0)
            start(0)
            inner_level(0, 1)

            def turn(i, last_out=True):
                main(i, True, last_out)
                tail_gate(i)
                front_rk(i + 1)
                front_zn_lo(i + 1)
                front_r(i + 1)
                front_lo(i + 1)
                start(i + 1)
                tail_gate1(i)
                inner_level(i + 1, 1)
                tail_rstd2(i)

            turn(0, last_out=False)
            with pool.Fori(1, TURNS - 1) as i:
                turn(i)
            main(TURNS - 1, False)
            tail_gate(TURNS - 1)
            tail_gate1(TURNS - 1)
            tail_rstd2(TURNS - 1)
            for g in both:
                add_residual(TURNS - 1, g)


def layout(inputs):
    f = np.float32
    a = {n: np.asarray(v) for n, v in inputs.items()}
    t = np.arange(P)
    masks = []
    for l in range(LEVELS):
        q = t[(t >> l) & 1 == 1]
        same = (t[:, None] >> (l + 1)) == (q[None, :] >> (l + 1))
        masks.append((same & ((t[:, None] >> l) & 1 == 0)).astype(f))
    parts = {
        "WxT": a["L0_attn_Wx"].T, "Ww": a["L0_attn_Ww"], "WvT0": a["L0_attn_Wv"].T, "Wo": a["L0_attn_Wo"],
        "Wk0": a["L0_attn_Wk"], "Wr0": a["L0_attn_Wr"],
        "routerT": a["L0_ffn_router_w"].T, "w1": a["L0_ffn_w1"],
        "w2": a["L0_ffn_w2"].reshape(E, W, P).transpose(1, 0, 2),
        "WqT": a["L1_attn_Wq"].T,
        "WkvT": np.concatenate([a["L1_attn_Wk"].T, a["L1_attn_Wv"].T], axis=1),
        "fWrT": a["L1_ffn_W_r"].T, "fWkT": a["L1_ffn_W_k"].T, "fWvT": a["L1_ffn_W_v"].T,
        "ln_g": a["L0_attn_ln_g"][:, None], "ln_b": a["L0_attn_ln_b"][:, None],
        "bw": a["L0_attn_bw"][:, None], "bq": a["L1_attn_bq"][:, None],
        "mu_r": a["L1_ffn_mu_r"][:, None], "mu_k": a["L1_ffn_mu_k"][:, None],
        "bkv": np.concatenate([a["L1_attn_bk"], a["L1_attn_bv"]])[None, :],
        "gamma": a["L1_attn_gamma"][None, :], "beta": a["L1_attn_beta"][None, :],
        "ident": np.eye(P, dtype=f), "level_mask": np.concatenate(masks, axis=1),
        "head_cols": (t[:, None] // HS == np.arange(NH)[None, :]).astype(f),
        "block_mask": (t[:, None] // AD == t[None, :] // AD).astype(f),
        "head_mask": (t[:, None] // AD == np.arange(AH)[None, :]).astype(f),
    }
    joined = {name: np.concatenate([parts[n].reshape(len(parts[n]), -1) for n in widths], axis=1)
            for name, widths in (("early", EARLY), ("late", LATE), ("rows", ROWS))}
    return {**joined, "w1": parts["w1"]}


def kernel(**inputs):
    import concourse.bacc as _bacc
    from concourse.bass_utils import run_bass_kernel_spmd as _run

    nc = _bacc.Bacc("TRN2", target_bir_lowering=False, num_devices=1)
    arrays = {"x": np.ascontiguousarray(inputs["L0_attn_x"])}
    for name, a in layout(inputs).items():
        arrays["in_" + name] = np.ascontiguousarray(a)
    dram = {n: nc.dram_tensor(n, a.shape, F32, kind="ExternalInput").ap() for n, a in arrays.items()}
    out = nc.dram_tensor("out", (B, T, P), F32, kind="ExternalOutput").ap()
    build(nc, dram["x"], {n[3:]: v for n, v in dram.items() if n != "x"}, out)
    r = _run(nc, [arrays], core_ids=[0])
    return r.results[0]["out"]
```
